# Optimizing a Trainium2 kernel written in Bass

```python
import numpy as np
import jax
import jax.numpy as jnp

def _softmax(x, axis=-1):
    return jax.nn.softmax(x, axis=axis)

def _gelu(x):
    return jax.nn.gelu(x, approximate=True)

def _silu(x):
    return jax.nn.silu(x)

def _sigmoid(x):
    return jax.nn.sigmoid(x)

def _layernorm(x, axis=-1, eps=1e-05):
    m = jnp.mean(x, axis=axis, keepdims=True)
    v = jnp.var(x, axis=axis, keepdims=True)
    return (x - m) / jnp.sqrt(v + eps)

def _scatter_add(tgt, idx, src, axis=0):
    return tgt.at[idx].add(src)

def _segment_sum(src, seg, n):
    return jax.ops.segment_sum(src, seg, n)
kernel_name = 'mk_gps_d1_gnn_r32_7e6e5c'

def setup_inputs(seed: int=0):
    np.random.seed(seed)
    _w = jnp.asarray

    def _rec_inputs():
        import jax
        import jax.numpy as jnp
        _gk = jax.random.key(seed)
        x = -0.0002117 + 1 * jax.random.normal(jax.random.fold_in(_gk, 1), (3125, 256), jnp.float32)
        src = jax.random.randint(jax.random.fold_in(_gk, 2), (50000,), 0, 3125, jnp.int32)
        dst = jax.random.randint(jax.random.fold_in(_gk, 3), (50000,), 0, 3125, jnp.int32)
        _o = jnp.argsort(dst, stable=True)
        src = src[_o]
        dst = dst[_o]
        edge_weight = jax.random.uniform(jax.random.fold_in(_gk, 12), (50000,), jnp.float32, 0.0, 0.03125)
        return (x, src, dst, edge_weight)
    x, src, dst, edge_weight = _rec_inputs()

    def _L0_gnn_setup():
        import jax, jax.numpy as jnp
        import numpy as np
        N_NODES = 3125
        N_EDGES = 100000
        D_IN = 256
        D_OUT = 256
        key = jax.random.key(seed)
        k1, k2, k3, k4, k5 = jax.random.split(key, 5)
        x = jax.random.normal(k1, (N_NODES, D_IN), dtype=jnp.float32)
        edge_row = jax.random.randint(k2, (N_EDGES,), 0, N_NODES, dtype=jnp.int32)
        edge_col = jax.random.randint(k3, (N_EDGES,), 0, N_NODES, dtype=jnp.int32)
        edge_val = jax.random.uniform(k4, (N_EDGES,), dtype=jnp.float32) / 32.0
        bound = 1.0 / np.sqrt(D_IN)
        weight = jax.random.uniform(k5, (D_IN, D_OUT), minval=-bound, maxval=bound, dtype=jnp.float32)
        return {'x': x, 'edge_row': edge_row, 'edge_col': edge_col, 'edge_val': edge_val, 'weight': weight}
    _L0_gnn_all = _L0_gnn_setup()
    _L0_gnn_in = {k: v for k, v in _L0_gnn_all.items() if k in ('weight',)}
    del _L0_gnn_all

    def _L0_mix_setup():
        import jax, jax.numpy as jnp
        import numpy as np
        D_MODEL = 256
        NUM_HEADS = 8
        DEPTH = D_MODEL // NUM_HEADS
        B, L = (32, 128)

        def _feature_map(x):
            return jax.nn.elu(x) + 1.0
        key = jax.random.key(seed)
        ks = jax.random.split(key, 9)
        sc = 1.0 / np.sqrt(D_MODEL)
        return {'x': jax.random.normal(ks[0], (B, L, D_MODEL), dtype=jnp.float32), 'wq': jax.random.normal(ks[1], (D_MODEL, D_MODEL), dtype=jnp.float32) * sc, 'bq': jnp.zeros((D_MODEL,), dtype=jnp.float32), 'wk': jax.random.normal(ks[2], (D_MODEL, D_MODEL), dtype=jnp.float32) * sc, 'bk': jnp.zeros((D_MODEL,), dtype=jnp.float32), 'wv': jax.random.normal(ks[3], (D_MODEL, D_MODEL), dtype=jnp.float32) * sc, 'bv': jnp.zeros((D_MODEL,), dtype=jnp.float32), 'wo': jax.random.normal(ks[4], (D_MODEL, D_MODEL), dtype=jnp.float32) * sc, 'bo': jnp.zeros((D_MODEL,), dtype=jnp.float32)}
    _L0_mix_all = _L0_mix_setup()
    _L0_mix_in = {k: v for k, v in _L0_mix_all.items() if k in ('wq', 'bq', 'wk', 'bk', 'wv', 'bv', 'wo', 'bo')}
    del _L0_mix_all

    def _L0_ffn_setup():
        import jax, jax.numpy as jnp
        import numpy as np
        E = 8
        K = 2
        D = 256
        H = 512
        DOUT = 256
        EPS = 1e-05
        key = jax.random.key(seed)
        ks = jax.random.split(key, 9)
        s = 0.02
        return {'x': jax.random.normal(ks[0], (4, 256, D), jnp.float32), 'gamma': 1.0 + 0.05 * jax.random.normal(ks[1], (D,), jnp.float32), 'beta': 0.05 * jax.random.normal(ks[2], (D,), jnp.float32), 'Wr': 0.01 * jax.random.normal(ks[3], (D, E), jnp.float32), 'br': jnp.zeros((E,), jnp.float32), 'W1': s * jax.random.normal(ks[4], (E, D, H), jnp.float32), 'b1': s * jax.random.normal(ks[5], (E, H), jnp.float32), 'W2': s * jax.random.normal(ks[6], (E, H, DOUT), jnp.float32), 'b2': s * jax.random.normal(ks[7], (E, DOUT), jnp.float32)}
    _L0_ffn_all = _L0_ffn_setup()
    _L0_ffn_in = {k: v for k, v in _L0_ffn_all.items() if k in ('gamma', 'beta', 'Wr', 'br', 'W1', 'b1', 'W2', 'b2')}
    del _L0_ffn_all
    return {'x': x, 'src': src, 'dst': dst, 'edge_weight': edge_weight, 'L0_gnn_weight': _L0_gnn_in['weight'], 'L0_mix_wq': _L0_mix_in['wq'], 'L0_mix_bq': _L0_mix_in['bq'], 'L0_mix_wk': _L0_mix_in['wk'], 'L0_mix_bk': _L0_mix_in['bk'], 'L0_mix_wv': _L0_mix_in['wv'], 'L0_mix_bv': _L0_mix_in['bv'], 'L0_mix_wo': _L0_mix_in['wo'], 'L0_mix_bo': _L0_mix_in['bo'], 'L0_ffn_gamma': _L0_ffn_in['gamma'], 'L0_ffn_beta': _L0_ffn_in['beta'], 'L0_ffn_Wr': _L0_ffn_in['Wr'], 'L0_ffn_br': _L0_ffn_in['br'], 'L0_ffn_W1': _L0_ffn_in['W1'], 'L0_ffn_b1': _L0_ffn_in['b1'], 'L0_ffn_W2': _L0_ffn_in['W2'], 'L0_ffn_b2': _L0_ffn_in['b2']}

def reference(x, src, dst, edge_weight, L0_gnn_weight, L0_mix_wq, L0_mix_bq, L0_mix_wk, L0_mix_bk, L0_mix_wv, L0_mix_bv, L0_mix_wo, L0_mix_bo, L0_ffn_gamma, L0_ffn_beta, L0_ffn_Wr, L0_ffn_br, L0_ffn_W1, L0_ffn_b1, L0_ffn_W2, L0_ffn_b2):
    import jax
    import jax.numpy as jnp

    def _L0_gnn_ref(x, edge_row, edge_col, edge_val, weight):
        import jax, jax.numpy as jnp
        import numpy as np
        N_NODES = 3125
        N_EDGES = 100000
        D_IN = 256
        D_OUT = 256
        gathered = edge_val[:, None] * x[edge_col]
        support = jax.ops.segment_sum(gathered, edge_row, num_segments=N_NODES)
        out = jax.nn.relu(support @ weight)
        return out

    def _L0_mix_ref(x, wq, bq, wk, bk, wv, bv, wo, bo):
        import jax, jax.numpy as jnp
        import numpy as np
        D_MODEL = 256
        NUM_HEADS = 8
        DEPTH = D_MODEL // NUM_HEADS
        B, L = (32, 128)

        def _feature_map(x):
            return jax.nn.elu(x) + 1.0
        b, l, _ = x.shape
        q = (x @ wq + bq).reshape(b, l, NUM_HEADS, DEPTH)
        k = (x @ wk + bk).reshape(b, l, NUM_HEADS, DEPTH)
        v = (x @ wv + bv).reshape(b, l, NUM_HEADS, DEPTH)
        q = _feature_map(q)
        k = _feature_map(k)
        kv = jnp.einsum('blhd,blhe->bhde', k, v)
        k_sum = jnp.sum(k, axis=1)
        qkv = jnp.einsum('blhd,bhde->blhe', q, kv)
        normalizer = jnp.einsum('blhd,bhd->blh', q, k_sum) + 1e-06
        out = qkv / normalizer[..., None]
        out = out.reshape(b, l, D_MODEL)
        return out @ wo + bo

    def _L0_ffn_ref(x, gamma, beta, Wr, br, W1, b1, W2, b2):
        import jax, jax.numpy as jnp
        import numpy as np
        E = 8
        K = 2
        D = 256
        H = 512
        DOUT = 256
        EPS = 1e-05
        mu = jnp.mean(x, axis=-1, keepdims=True)
        var = jnp.mean(jnp.square(x - mu), axis=-1, keepdims=True)
        xn = (x - mu) * jax.lax.rsqrt(var + EPS) * gamma + beta
        logits = jnp.einsum('bsd,de->bse', xn, Wr) + br
        top_vals, top_idx = jax.lax.top_k(logits, K)
        w = jax.nn.softmax(top_vals, axis=-1)
        w_full = jnp.einsum('bsk,bske->bse', w, jax.nn.one_hot(top_idx, E, dtype=w.dtype))
        y = jnp.zeros(x.shape[:-1] + (DOUT,), x.dtype)
        for e in range(E):
            h = jax.nn.gelu(jnp.einsum('bsd,dh->bsh', xn, W1[e]) + b1[e], approximate=False)
            y_e = jnp.einsum('bsh,hd->bsd', h, W2[e]) + b2[e]
            y = y + y_e * w_full[..., e, None]
        return y
    xn = _layernorm(x, axis=-1)
    x = x + _L0_gnn_ref(xn, src, dst, edge_weight, L0_gnn_weight) + _L0_mix_ref(xn[None], L0_mix_wq, L0_mix_bq, L0_mix_wk, L0_mix_bk, L0_mix_wv, L0_mix_bv, L0_mix_wo, L0_mix_bo)[0]
    x = x + _L0_ffn_ref(_layernorm(x, axis=-1)[None], L0_ffn_gamma, L0_ffn_beta, L0_ffn_Wr, L0_ffn_br, L0_ffn_W1, L0_ffn_b1, L0_ffn_W2, L0_ffn_b2)[0]
    return x

_drawn_inputs = setup_inputs


def setup_inputs(seed=0):
    import zlib

    import numpy as np

    out = dict(_drawn_inputs(seed))
    spreads = {'L0_mix_bq': (0.0, 2.0),
     'L0_mix_bk': (0.0, 2.0),
     'L0_mix_bv': (0.0, 0.1),
     'L0_mix_bo': (0.0, 0.1),
     'L0_ffn_br': (0.0, 0.1)}
    factors = {'edge_weight': 3.947,
     'L0_mix_wq': 8.0,
     'L0_mix_wk': 5.779,
     'L0_mix_wv': 2.83,
     'L0_ffn_gamma': 6.254,
     'L0_ffn_beta': 4.997,
     'L0_ffn_b1': 8.0,
     'L0_ffn_b2': 4.305}
    for name, (base, spread) in spreads.items():
        noise = np.random.default_rng([zlib.crc32(name.encode()), seed]).standard_normal(out[name].shape)
        drawn = base * np.exp(spread * noise) if base else spread * noise
        out[name] = jnp.asarray(drawn.astype(out[name].dtype))
    for name, factor in factors.items():
        out[name] = (out[name] * factor).astype(out[name].dtype)
    return out
```

```python
from contextlib import ExitStack

import concourse.bass as bass
from concourse import mybir

F32, F32R, I32, U32 = mybir.dt.float32, mybir.dt.float32r, mybir.dt.int32, mybir.dt.uint32
ALU = mybir.AluOpType
ACT = mybir.ActivationFunctionType
AX = mybir.AxisListType

P = 128
N, D = 3125, 256
T = 125
NT = N // T
E = 50000
J = -(-E // P)
LAST = E - (P - 1) * J
C = 17
CAP = C * P
NB = NT * C
CH = J // C
HEADS, HD = 8, 32
NE, HID = 8, 512
HC = HID // P
KD = D // P
W2T = 2 * T
PAIRS = NT // 2
EPS = 1e-5
RSQRT_BITS = 0x5F3759DF
assert CH * C == J and CH % 2 == 1 and NT % 2 == 1 and NT * T == N


def apart(eng, passed):
    eng.sem_inc(passed, 1)


class Steps:

    def __init__(self, eng, sem, before=0):
        self.eng, self.sem, self.before, self.n = eng, sem, before, 0

    def __call__(self, ins, passed=None):
        self.n += 1
        ins.then_inc(self.sem, 1)
        self.eng.wait_ge(self.sem, self.before + self.n)
        if passed is not None:
            apart(self.eng, passed)


def rsqrt(eng, s, v, y, a):
    s(eng.tensor_scalar(y.bitcast(I32), v.bitcast(I32), 1, None, ALU.logical_shift_right))
    s(eng.tensor_scalar(y.bitcast(I32), y.bitcast(I32), -1.0, float(RSQRT_BITS), ALU.mult, ALU.add))
    for _ in range(3):
        s(eng.scalar_tensor_tensor(a, y, -0.5, y, ALU.mult, ALU.mult))
        s(eng.tensor_tensor(a, a, v, ALU.mult))
        s(eng.scalar_tensor_tensor(y, a, 1.5, y, ALU.add, ALU.mult))


RSQRT_STEPS = 11


def build(nc, x, src, dst, edge_weight, w_gnn, wq, bq, wk, bk, wv, bv, wo, bo, gamma, beta, Wr, br,
          W1, b1, W2, b2, out):
    ctx = ExitStack()
    with ctx:
        def sb(name, shape, dt=F32, where=ctx):
            return where.enter_context(nc.sbuf_tensor(name, shape, dt))

        def sem(name):
            return ctx.enter_context(nc.semaphore(name))

        slots = nc.dram_tensor("slots", (P * NB, 4), F32, kind="Internal").ap()
        slots_by_lane = slots.rearrange("(p b) r -> p b r", p=P)
        table = nc.dram_tensor("table", (N, D), F32, kind="Internal").ap()
        mixed = nc.dram_tensor("mixed", (N, D), F32, kind="Internal").ap()
        extra = nc.dram_tensor("extra", (N, D), F32, kind="Internal").ap()

        iota_row = sb("iota_row", [P, T])
        ident = sb("ident", [P, P])
        rec = sb("rec", [P, J, 4])
        over_w = sb("over_w", [P, J])
        src_f = sb("src_f", [P, J])

        with ExitStack() as early:
            src_i = sb("src_i", [P, J], I32, early)
            dst_i = sb("dst_i", [P, J], I32, early)
            weight = sb("weight", [P, J], F32, early)
            tile_i = sb("tile_i", [P, J], I32, early)
            tile_f = sb("tile_f", [P, J], F32, early)
            rest = sb("rest", [P, J], F32, early)
            zeros = sb("zeros", [P, 1700], F32, early)
            mask = sb("mask", [P, NT, J], F32, early)
            seen = sb("seen", [P, NT, J], F32, early)
            rank = sb("rank", [P, J], F32, early)
            above = sb("above", [P, P], F32, early)
            totals = sb("totals", [P, NT], F32, early)
            before = sb("before", [P, NT], F32, early)
        w1h = sb("w1h", [P, NE, KD, HID], F32R)
        w1l = sb("w1l", [P, NE, KD, HID], F32R)
        w2h = sb("w2h", [P, NE, HC, D], F32R)
        w2l = sb("w2l", [P, NE, HC, D], F32R)

        gamma_s, beta_s = sb("gamma_s", [P, D]), sb("beta_s", [P, D])
        br_s = sb("br_s", [P, NE])
        b1_s = sb("b1_s", [P, NE, HC])
        b2_s = sb("b2_s", [NE, D])
        wr_s = sb("wr_s", [P, KD, NE])
        wr_h = sb("wr_h", [P, KD, NE], F32R)
        wr_l = sb("wr_l", [P, KD, NE], F32R)

        with ExitStack() as mid:
            q_t = sb("q_t", [P, KD, N], F32, mid)
            wq_s, wk_s, wv_s, wo_s, wg_s = (sb(n, [P, KD, D], F32, mid)
                                            for n in ("wq_s", "wk_s", "wv_s", "wo_s", "wg_s"))
            bk_s, bv_s, bo_s = (sb(n, [P, D], F32, mid) for n in ("bk_s", "bv_s", "bo_s"))
            bq_s = sb("bq_s", [P, KD], F32, mid)
            x_in = sb("x_in", [P, 2, D], F32, mid)
            xn = sb("xn", [P, D], F32, mid)
            xn_t = sb("xn_t", [P, KD, T], F32, mid)
            stat1 = sb("stat1", [P, 6], F32, mid)
            mv1 = sb("mv1", [P, 2], F32, mid)
            rs1 = sb("rs1", [P, 4], F32, mid)
            q_exp = sb("q_exp", [P, KD, T], F32, mid)
            q_pos = sb("q_pos", [P, KD, T], F32, mid)
            k_z = sb("k_z", [P, D], F32, mid)
            k_exp = sb("k_exp", [P, D], F32, mid)
            k_map = sb("k_map", [P, D], F32, mid)
            v_one = sb("v_one", [P, KD, P + 1], F32, mid)
            g_out = sb("g_out", [P, D], F32, mid)
            kv_s = sb("kv_s", [P, KD, P + HEADS // KD], F32, mid)
            q_now = sb("q_now", [P, KD, T], F32, mid)
            norm = sb("norm", [P, HEADS], F32, mid)
            attn = sb("attn", [P, D], F32, mid)
            attn_t = sb("attn_t", [P, KD, T], F32, mid)
            mix_out = sb("mix_out", [P, D], F32, mid)
            rec_buf = sb("rec_buf", [P, 2, C, 4], F32, mid)
            stage = sb("stage", [P, 2, NE // 4 * D * 2], F32, mid)
        rows = sb("rows", [P, C, D])
        onehot = sb("onehot", [P, C, T])
        slot_rec = sb("slot_rec", [P, 2, C, 4])
        mixed_in = sb("mixed_in", [P, 2, D])
        extra_in = sb("extra_in", [P, 2, D])
        x2 = sb("x2", [P, 2, D])
        z = sb("z", [P, 2, D])
        stat = sb("stat", [P, 2, 6])
        mv = sb("mv", [P, 2, 2])
        rs = sb("rs", [P, 3, 2])
        xf_h = sb("xf_h", [P, KD, W2T], F32R)
        xf_l = sb("xf_l", [P, KD, W2T], F32R)
        h = sb("h", [P, HC, W2T])
        h_h = sb("h_h", [P, 2, HC, W2T], F32R)
        h_l = sb("h_l", [P, 2, HC, W2T], F32R)
        logit = sb("logit", [P, 2, NE])
        top = sb("top", [P, 2, NE])
        top_at = sb("top_at", [P, 2, NE], U32)
        top_f = sb("top_f", [P, 2, NE])
        share = sb("share", [P, 2, 4])
        gate = sb("gate", [P, 2, NE])
        gate_t = sb("gate_t", [NE, 2, T])
        y = sb("y", [P, 2, D])
        hp = ctx.enter_context(nc.psum_tensor("hp", [P, 2, HC, 256], F32))
        yp = ctx.enter_context(nc.psum_tensor("yp", [P, 2, 2, D], F32))
        agg = ctx.enter_context(nc.psum_tensor("agg", [P, 2, D], F32))
        misc = ctx.enter_context(nc.psum_tensor("misc", [P, 512], F32))
        banks = hp[:, :, :, :].rearrange("p a (b c) n -> p (a b) (c n)", b=2)
        q_p = banks[:, 0, 0:W2T].rearrange("p (c n) -> p c n", c=KD)
        k_p, v_p = banks[:, 1, 0:D], banks[:, 1, D:2 * D]
        g_p = banks[:, 2, 0:D]
        mix_p = banks[:, 2, 0:D]
        xn_tp = banks[:, 3, 0:W2T].rearrange("p (c n) -> p c n", c=KD)
        before_p = banks[:, 3, 0:NT]
        NK = P + HEADS // KD
        attn_p = banks[:, 0, 0:KD * NK].rearrange("p (c n) -> p c n", c=KD)
        kv_p = [yp[:, c, :, :].rearrange("p a n -> p (a n)")[:, 0:P + 1] for c in range(KD)]

        (pads_set, edges_in, zeros_set, zeros_out, consts_set, totals_done, before_mm, records_set,
         dve_step) = map(sem, ("pads_set", "edges_in", "zeros_set", "zeros_out", "consts_set",
                               "totals_done", "before_mm", "records_set", "dve_step"))
        chunk_in = [sem(f"chunk_in{i}") for i in range(2)]
        chunk_out = [sem(f"chunk_out{i}") for i in range(2)]
        (small_in, x_loaded0, x_loaded1, x_normed, xn_turned, xn_t_set, proj_done, q_exped, k_zed,
         k_exped, k_set, v_set, q_set, g_copied, g_stored, kv_added) = map(sem, (
             "small_in", "x_loaded0", "x_loaded1", "x_normed", "xn_turned", "xn_t_set", "proj_done",
             "q_exped", "k_zed", "k_exped", "k_set", "v_set", "q_set", "g_copied", "g_stored",
             "kv_added"))
        x_loaded = [x_loaded0, x_loaded1]
        kv_total, kv_ready, split_in0, split_in1, split_high, split_low = map(sem, (
            "kv_total", "kv_ready", "split_in0", "split_in1", "split_high", "split_low"))
        split_in = [split_in0, split_in1]
        q_copied, attn_mm, attn_set, attn_turned, attn_t_set, mix_mm, mix_set, mix_stored = map(
            sem, ("q_copied", "attn_mm", "attn_set", "attn_turned", "attn_t_set", "mix_mm",
                  "mix_set", "mix_stored"))
        slots_in = [sem(f"slots_in{i}") for i in range(2)]
        rest_in = [sem(f"rest_in{i}") for i in range(2)]
        row_in = [sem(f"row_in{c}") for c in range(C)]
        onehot_set, block_added, x2_set, normed, turned, xf_high, xf_low = map(sem, (
            "onehot_set", "block_added", "x2_set", "normed", "turned", "xf_high",
            "xf_low"))
        (logits_mm, diff_set, tanh_set, gate_set, gate_turned, gate_copied, bias_mm, y_begun,
         hidden_mm, h_set, h_high, h_split, expert_mm, y_added, y_stored) = map(sem, (
             "logits_mm", "diff_set", "tanh_set", "gate_set", "gate_turned", "gate_copied",
             "bias_mm", "y_begun", "hidden_mm", "h_set", "h_high", "h_split", "expert_mm",
             "y_added", "y_stored"))
        stage2_done = sem("stage2_done")
        pool_passed, dve_passed = sem("pool_passed"), sem("dve_passed")
        q_pos_set, k_pos_set = sem("q_pos_set"), sem("k_pos_set")
        wr_split = sem("wr_split")

        block = ctx.enter_context(nc.Block())
        SMALL = 16 * 15

        def by_chunk(w):
            return w.rearrange("(k p) n -> p k n", p=P)

        def to_rows(b):
            return b.rearrange("(a n) -> a n", a=1).to_broadcast([P, b.shape[0]])

        @block.sync
        def _(sp):
            sp.wait_ge(pads_set, 3)
            for t, v in ((src_i, src), (dst_i, dst), (weight, edge_weight)):
                sp.dma_start(t[0:P - 1, :], v[0:(P - 1) * J].rearrange("(p j) -> p j", p=P - 1)).then_inc(edges_in, 16)
                sp.dma_start(t[P - 1:P, 0:LAST], v[(P - 1) * J:E].rearrange("(p j) -> p j", p=1)).then_inc(edges_in, 16)
            sp.wait_ge(zeros_set, 1)
            sp.dma_start(slots_by_lane.rearrange("p b r -> p (b r)"), zeros[:, 0:NB * 4]).then_inc(zeros_out, 16)
            for i in range(4):
                w = N * D // T // 4
                sp.dma_start(extra.rearrange("(p a) n -> p (a n)", p=T)[:, i * w:(i + 1) * w],
                             zeros[0:T, 0:w]).then_inc(zeros_out, 16)

            def chunk(c, b, k):
                sp.dma_start(rec_buf[:, b, :, :].rearrange("p c r -> p (c r)"),
                             rec[:, bass.ds(c * C, C), :].rearrange("p c r -> p (c r)"))\
                    .then_inc(chunk_in[b], 16)

            sp.wait_ge(records_set, 1)
            chunk(0, 0, 0)
            chunk(1, 1, 0)
            with sp.Fori(1, CH // 2) as i:
                for b in range(2):
                    sp.wait_ge(chunk_out[b], 16 * C * i)
                    chunk(2 * i + b, b, i)
            sp.wait_ge(chunk_out[0], 16 * C * (CH // 2))
            chunk(CH - 1, 0, CH // 2)

            sp.wait_ge(chunk_out[0], 16 * C * (CH // 2 + 1))
            sp.wait_ge(chunk_out[1], 16 * C * (CH // 2))
            sp.wait_ge(zeros_out, 16 * 5)
            sp.wait_ge(mix_stored, 16 * NT)
            sp.wait_ge(g_stored, 16 * NT)

            def load(t, b, k, first=False):
                if not first:
                    sp.wait_ge(block_added, (t - 1) * C)
                sp.dma_start(slot_rec[:, b, :, :].rearrange("p c r -> p (c r)"),
                             slots_by_lane[:, bass.ds(t * C, C), :].rearrange("p c r -> p (c r)"))\
                    .then_inc(slots_in[b], 16)
                if not first:
                    sp.wait_ge(x2_set, t - 1)
                sp.dma_start(mixed_in[0:T, b, :], mixed[bass.ds(t * T, T), :]).then_inc(rest_in[b], 16)
                sp.dma_start(extra_in[0:T, b, :], extra[bass.ds(t * T, T), :]).then_inc(rest_in[b], 16)

            def store(p, b):
                sp.dma_start(out[bass.ds((2 * p + b) * T, T), :], y[0:T, b, :]).then_inc(y_stored, 16)

            load(0, 0, 0, True)
            load(1, 1, 0, True)
            with sp.Fori(0, PAIRS - 1) as p:
                for b in range(2):
                    load(2 * p + 2 + b, b, p + 1)
                sp.wait_ge(y_added, NE * (p + 1))
                for b in range(2):
                    store(p, b)
            load(NT - 1, 0, PAIRS)
            sp.wait_ge(y_added, NE * PAIRS)
            for b in range(2):
                store(PAIRS - 1, b)
            sp.wait_ge(y_added, NE * (PAIRS + 1))
            store(PAIRS, 0)
            sp.wait_ge(y_stored, 16 * NT)

        @block.gpsimd
        def _(pool):
            pool.iota(iota_row[:, :], [[1, T]], base=0, channel_multiplier=0,
                      allow_small_or_imprecise_dtypes=True).then_inc(consts_set, 1)
            pool.memset(ident[:, :], 0.0).then_inc(consts_set, 1)
            pool.memset(above[:, :], 1.0).then_inc(consts_set, 1)
            pool.wait_ge(consts_set, 3)
            pool.affine_select(out=ident[:, :], in_=ident[:, :], compare_op=ALU.not_equal, fill=1.0,
                               base=0, pattern=[[-1, P]], channel_multiplier=1).then_inc(consts_set, 1)
            pool.affine_select(out=above[:, :], in_=above[:, :], compare_op=ALU.is_gt, fill=0.0,
                               base=0, pattern=[[1, P]], channel_multiplier=-1).then_inc(consts_set, 1)

            pool.wait_ge(zeros_out, 16 * 5)

            def scatter(b, k):
                pool.wait_ge(chunk_in[b], 16 * (k + 1))
                apart(pool, pool_passed)
                for c in range(C):
                    pool.indirect_dma_start(
                        slots, bass.IndirectOffsetOnAxis(ap=rec_buf[:, b, c, 3:4].bitcast(I32), axis=0),
                        rec_buf[:, b, c, :], None, bounds_check=P * NB - 1, oob_is_err=False)\
                        .then_inc(chunk_out[b], 16)

            with pool.Fori(0, CH // 2) as i:
                for b in range(2):
                    scatter(b, i)
            scatter(0, CH // 2)

            pool.wait_ge(stage2_done, 1)
            pool.wait_ge(g_stored, 16 * NT)

            def gather(t, b, k, first=False):
                pool.wait_ge(slots_in[b], 16 * (k + 1))
                apart(pool, pool_passed)
                for c in range(C):
                    if not first:
                        pool.wait_ge(block_added, (t - 1) * C + c + 1)
                        apart(pool, pool_passed)
                    pool.indirect_dma_start(
                        rows[:, c, :], None, table,
                        bass.IndirectOffsetOnAxis(ap=slot_rec[:, b, c, 2:3].bitcast(I32), axis=0))\
                        .then_inc(row_in[c], 16)

            gather(0, 0, 0, True)
            gather(1, 1, 0)
            with pool.Fori(1, PAIRS) as p:
                for b in range(2):
                    gather(2 * p + b, b, p)
            gather(NT - 1, 0, PAIRS)

        @block.scalar
        def _(act):
            for w, t in ((wq, wq_s), (wk, wk_s), (wv, wv_s), (wo, wo_s), (w_gnn, wg_s)):
                act.dma_start(t[:, :, :], by_chunk(w)).then_inc(small_in, 16)
            for b, t in ((bk, bk_s), (bv, bv_s), (bo, bo_s), (gamma, gamma_s), (beta, beta_s), (br, br_s)):
                act.dma_start(t[:, :], to_rows(b)).then_inc(small_in, 16)
            with nc.allow_non_contiguous_dma(reason="a few thousand numbers, once"):
                act.dma_start(bq_s[:, :], bq.rearrange("(k p) -> p k", p=P)).then_inc(small_in, 16)
                act.dma_start(b1_s[:, :, :], b1.rearrange("e (c p) -> p e c", p=P)).then_inc(small_in, 16)
            act.dma_start(b2_s[:, :], b2).then_inc(small_in, 16)
            act.dma_start(wr_s[:, :, :], by_chunk(Wr)).then_inc(small_in, 16)
            act.wait_ge(small_in, SMALL)

            def load_x(t, b):
                act.dma_start(x_in[0:T, b, :], x[bass.ds(t * T, T), :]).then_inc(x_loaded[b], 16)

            def sweep1(t, b, last=False):
                act.wait_ge(xn_turned, t + 1)
                act.activation(xn_t[:, :, :], xn_tp, ACT.Copy).then_inc(xn_t_set, 1)
                if not last:
                    load_x(t + 1, 1 - b)
                act.wait_ge(proj_done, t + 1)
                for c in range(KD):
                    act.activation(q_exp[:, c, :], q_p[:, c, :], ACT.Exp, bias=bq_s[:, c:c + 1]).then_inc(q_exped, 1)
                act.wait_ge(g_stored, 16 * t) if not isinstance(t, int) or t else None
                act.activation(g_out[0:T, :], g_p[0:T, :], ACT.Copy).then_inc(g_copied, 1)
                act.wait_ge(k_zed, t + 1)
                act.activation(k_exp[0:T, :], k_z[0:T, :], ACT.Exp).then_inc(k_exped, 1)
                act.wait_ge(g_copied, t + 1)
                act.dma_start(table[bass.ds(t * T, T), :], g_out[0:T, :]).then_inc(g_stored, 16)

            load_x(0, 0)
            sweep1(0, 0)
            with act.Fori(0, (NT - 3) // 2) as i:
                sweep1(2 * i + 1, 1)
                sweep1(2 * i + 2, 0)
            sweep1(NT - 2, 1)
            sweep1(NT - 1, 0, last=True)

            def stage_in(e):
                act.dma_start(stage[:, 0, :].rearrange("p (k n) -> p k n", k=KD),
                              W1[bass.ds(e, 1), :, :].rearrange("e (k p) n -> p (e k) n", p=P)).then_inc(split_in[0], 16)
                act.dma_start(stage[:, 1, :].rearrange("p (k n) -> p k n", k=HC),
                              W2[bass.ds(e, 1), :, :].rearrange("e (k p) n -> p (e k) n", p=P)).then_inc(split_in[1], 16)

            act.wait_ge(records_set, 1)
            act.wait_ge(zeros_out, 16 * 5)
            with act.Fori(0, NE) as e:
                act.wait_ge(split_low, 2 * e)
                stage_in(e)
                for i, w in enumerate((w1h, w2h)):
                    act.wait_ge(split_in[i], 16 * (e + 1))
                    act.activation(w[:, bass.ds(e, 1), :, :].rearrange("p e k n -> p (e k n)"),
                                   stage[:, i, :], ACT.Copy).then_inc(split_high, 1)
            act.activation(wr_h[:, :, :], wr_s[:, :, :], ACT.Copy).then_inc(wr_split, 1)

            def sweep2(t, b, last=False):
                act.activation(q_now[:, :, :], q_t[:, :, bass.ds(t * T, T)], ACT.Copy).then_inc(q_copied, 1)
                if not last:
                    if not isinstance(t, int) or t:
                        act.wait_ge(mix_set, t)
                    load_x(t + 1, b)
                act.wait_ge(attn_turned, t + 1)
                act.activation(attn_t[:, :, :], xn_tp, ACT.Copy).then_inc(attn_t_set, 1)
                act.wait_ge(mix_set, t + 1)
                act.dma_start(mixed[bass.ds(t * T, T), :], mix_out[0:T, :]).then_inc(mix_stored, 16)

            act.wait_ge(x_normed, NT)
            load_x(0, 1)
            act.wait_ge(q_set, NT)
            sweep2(0, 0)
            with act.Fori(0, (NT - 3) // 2) as i:
                sweep2(2 * i + 1, 1)
                sweep2(2 * i + 2, 0)
            sweep2(NT - 2, 1)
            sweep2(NT - 1, 0, last=True)

            def halves(p):
                act.wait_ge(turned, p + 1)
                act.activation(xf_h[:, :, :].rearrange("p k n -> p (k n)"), misc[:, 0:KD * W2T], ACT.Copy).then_inc(xf_high, 1)

            def expert(p, e, n):
                x_ = p * NE + e
                act.wait_ge(hidden_mm, x_ + 1)
                for c in range(HC):
                    if c == 0 and (e or not isinstance(p, int) or p):
                        act.wait_ge(h_split, x_)
                    act.activation(h[:, c, 0:n], hp[:, e % 2, c, 0:n], ACT.Gelu,
                                   bias=b1_s[:, e, c:c + 1]).then_inc(h_set, 1)

            def pair(p, tiles, nxt):
                for e in range(NE):
                    if e == 0:
                        act.wait_ge(diff_set, p + 1)
                        act.activation(share[0:T, 0:tiles, 1:2], share[0:T, 0:tiles, 0:1], ACT.Tanh, scale=0.5).then_inc(tanh_set, 1)
                    expert(p, e, W2T if tiles == 2 else T + 1)
                    if e == 1:
                        act.wait_ge(gate_turned, p + 1)
                        act.activation(gate_t[:, 0:tiles, :], misc[0:NE, 0:tiles * T].rearrange("p (b n) -> p b n", b=tiles), ACT.Copy).then_inc(gate_copied, 1)
                if nxt:
                    halves(p + 1)

            halves(0)
            with act.Fori(0, PAIRS) as p:
                pair(p, 2, 2)
            pair(PAIRS, 1, 0)

        @block.tensor
        def _(pe):
            pe.wait_ge(consts_set, 5)
            pe.wait_ge(totals_done, 1)
            pe.matmul(before_p, above[:, :], totals[:, :], start=True, stop=True).then_inc(before_mm, 1)

            pe.wait_ge(small_in, SMALL)
            pe.wait_ge(k_set, 1)
            pe.wait_ge(v_set, 1)
            for c in range(KD):
                pe.matmul(kv_p[c], k_map[0:T, c * P:(c + 1) * P], v_one[0:T, c, :], start=True, stop=False,
                          skip_group_check=True).then_inc(kv_added, 1)
            pe.wait_ge(before_mm, 1)

            with pe.Fori(0, NT) as t:
                pe.wait_ge(x_normed, t + 1)
                pe.wait_ge(xn_t_set, t)
                for c in range(KD):
                    m = pe.transpose(xn_tp[:, c, :], xn[0:T, c * P:(c + 1) * P], ident[0:T, 0:T])
                m.then_inc(xn_turned, 1)
                pe.wait_ge(xn_t_set, t + 1)
                pe.wait_ge(q_set, t)
                pe.wait_ge(k_set, t + 1)
                pe.wait_ge(v_set, t + 1)
                pe.wait_ge(g_copied, t)
                for c in range(KD):
                    for k in range(KD):
                        pe.matmul(q_p[:, c, :], wq_s[:, k, c * P:(c + 1) * P], xn_t[:, k, :], start=k == 0, stop=k == KD - 1)
                for o, w in ((k_p, wk_s), (v_p, wv_s), (g_p, wg_s)):
                    for k in range(KD):
                        m = pe.matmul(o[0:T, :], xn_t[:, k, :], w[:, k, :], start=k == 0, stop=k == KD - 1)
                m.then_inc(proj_done, 1)
                pe.wait_ge(k_set, t + 2)
                pe.wait_ge(v_set, t + 2)
                for c in range(KD):
                    m = pe.matmul(kv_p[c], k_map[0:T, c * P:(c + 1) * P], v_one[0:T, c, :], start=False, stop=False,
                                  skip_group_check=True)
                m.then_inc(kv_added, 1)
            pe.wait_ge(kv_ready, 1)
            for c in range(KD):
                m = pe.matmul(kv_p[c], k_map[0:T, c * P:(c + 1) * P], v_one[0:T, c, :], start=False, stop=True,
                              skip_group_check=True)
            m.then_inc(kv_total, 1)

            pe.wait_ge(kv_ready, 2)
            with pe.Fori(0, NT) as t:
                pe.wait_ge(q_copied, t + 1)
                pe.wait_ge(attn_set, t)
                for c in range(KD):
                    m = pe.matmul(attn_p[0:T, c, :], q_now[:, c, :], kv_s[:, c, :], start=True, stop=True)
                m.then_inc(attn_mm, 1)
                pe.wait_ge(attn_set, t + 1)
                pe.wait_ge(attn_t_set, t)
                for c in range(KD):
                    m = pe.transpose(xn_tp[:, c, :], attn[0:T, c * P:(c + 1) * P], ident[0:T, 0:T])
                m.then_inc(attn_turned, 1)
                pe.wait_ge(attn_t_set, t + 1)
                pe.wait_ge(mix_set, t)
                for k in range(KD):
                    m = pe.matmul(mix_p[0:T, :], attn_t[:, k, :], wo_s[:, k, :], start=k == 0, stop=k == KD - 1)
                m.then_inc(mix_mm, 1)

            def three(o, lh, ll, rh, rl, start, stop):
                pe.matmul(o, lh, rh, start=start, stop=False)
                pe.matmul(o, lh, rl, start=False, stop=False)
                return pe.matmul(o, ll, rh, start=False, stop=stop)

            def add_block(t, b, c):
                if b == 0 and c == 0 and (not isinstance(t, int) or t):
                    pe.wait_ge(x2_set, t)
                pe.wait_ge(onehot_set, t * C + c + 1)
                pe.wait_ge(row_in[c], 16 * (t + 1))
                m = pe.matmul(agg[0:T, b, :], onehot[:, c, :], rows[:, c, :], start=c == 0, stop=c == C - 1)
                m.then_inc(block_added, 1)

            def turn(p, tiles):
                pe.wait_ge(normed, p + 1)
                if not isinstance(p, int) or p:
                    pe.wait_ge(y_begun, p)
                for b in range(tiles):
                    for k in range(KD):
                        m = pe.transpose(misc[:, (k * 2 + b) * T:(k * 2 + b + 1) * T],
                                         z[0:T, b, k * P:(k + 1) * P], ident[0:T, 0:T])
                m.then_inc(turned, 1)

            def hidden(p, e, n):
                x_ = p * NE + e
                if e >= 2:
                    pe.wait_ge(h_set, HC * (x_ - 1))
                for c in range(HC):
                    for k in range(KD):
                        m = three(hp[:, e % 2, c, 0:n], w1h[:, e, k, c * P:(c + 1) * P], w1l[:, e, k, c * P:(c + 1) * P],
                                  xf_h[:, k, 0:n], xf_l[:, k, 0:n], k == 0, k == KD - 1)
                m.then_inc(hidden_mm, 1)

            def output(p, e, tiles):
                x_ = p * NE + e
                pe.wait_ge(h_split, x_ + 1)
                pe.wait_ge(y_added, x_ - 1 if e else x_)
                for b in range(tiles):
                    for c in range(HC):
                        m = three(yp[0:T, e % 2, b, :], h_h[:, e % 2, c, b * T:(b + 1) * T], h_l[:, e % 2, c, b * T:(b + 1) * T],
                                  w2h[:, e, c, :], w2l[:, e, c, :], c == 0, c == HC - 1)
                m.then_inc(expert_mm, 1)

            def pair(p, tiles, nxt):
                n = W2T if tiles == 2 else T + 1
                todo = [(b, c) for b in range(nxt) for c in range(C)]
                part = -(-len(todo) // 6)
                pe.wait_ge(xf_high, p + 1)
                pe.wait_ge(xf_low, p + 1)
                for b in range(tiles):
                    for k in range(KD):
                        m = three(misc[0:T, b * NE:(b + 1) * NE], xf_h[:, k, b * T:(b + 1) * T], xf_l[:, k, b * T:(b + 1) * T],
                                  wr_h[:, k, :], wr_l[:, k, :], k == 0, k == KD - 1)
                m.then_inc(logits_mm, 1)
                for e in range(NE):
                    hidden(p, e, n)
                    if e == 1:
                        pe.wait_ge(gate_set, p + 1)
                        for b in range(tiles):
                            m = pe.transpose(misc[0:NE, b * T:(b + 1) * T], gate[0:T, b, :], ident[0:T, 0:T])
                        m.then_inc(gate_turned, 1)
                    for b, c in todo[e * part:(e + 1) * part]:
                        add_block(2 * p + 2 + b, b, c)
                    if e == 1:
                        pe.wait_ge(gate_copied, p + 1)
                        for b in range(tiles):
                            m = pe.matmul(misc[0:T, b * D:(b + 1) * D], gate_t[:, b, :], b2_s[:, :], start=True, stop=True)
                        m.then_inc(bias_mm, 1)
                    if e:
                        output(p, e - 1, tiles)
                output(p, NE - 1, tiles)
                if nxt:
                    turn(p + 1, nxt)

            pe.wait_ge(wr_split, 2)
            pe.wait_ge(split_low, 2 * NE)
            for b in range(2):
                for c in range(C):
                    add_block(b, b, c)
            turn(0, 2)
            with pe.Fori(0, PAIRS - 1) as p:
                pair(p, 2, 2)
            pair(PAIRS - 1, 2, 1)
            pair(PAIRS, 1, 0)

        @block.vector
        def _(dve):
            s = Steps(dve, dve_step)
            dve.memset(src_i[96:P, LAST:J], N - 1).then_inc(pads_set, 1)
            dve.memset(dst_i[96:P, LAST:J], 0).then_inc(pads_set, 1)
            dve.memset(weight[96:P, LAST:J], 0.0).then_inc(pads_set, 1)
            dve.memset(zeros[:, :], 0.0).then_inc(zeros_set, 1)
            dve.memset(k_map[:, :], 0.0).then_inc(k_set, 1)
            dve.memset(v_one[:, :, :], 1.0).then_inc(v_set, 1)
            dve.memset(kv_s[:, :, :], 0.0).then_inc(pads_set, 1)
            dve.wait_ge(edges_in, 16 * 6)

            dve.tensor_copy(rec[:, :, 1], weight[:, :])
            dve.tensor_copy(rec[:, :, 2].bitcast(I32), dst_i[:, :])
            s(dve.tensor_copy(src_f[:, :], src_i[:, :]))
            s(dve.tensor_scalar(tile_i[:, :], src_f[:, :], 1.0 / T, 0.5 / T, ALU.mult, ALU.add))
            s(dve.tensor_copy(tile_f[:, :], tile_i[:, :]))
            s(dve.scalar_tensor_tensor(rest[:, :], tile_f[:, :], -float(T), src_f[:, :], ALU.mult, ALU.add))
            s(dve.scalar_tensor_tensor(tile_f[:, :], rest[:, :], float(T), tile_f[:, :], ALU.is_ge, ALU.add))
            s(dve.scalar_tensor_tensor(tile_f[:, :], rest[:, :], 0.0, tile_f[:, :], ALU.is_ge, ALU.add))
            s(dve.tensor_scalar(tile_f[:, :], tile_f[:, :], -1.0, None, ALU.add))
            s(dve.scalar_tensor_tensor(rec[:, :, 0], tile_f[:, :], -float(T), src_f[:, :], ALU.mult, ALU.add))
            for t in range(NT):
                m = dve.tensor_scalar(mask[:, t, :], tile_f[:, :], float(t), None, ALU.is_equal)
            s(m)
            for t in range(NT):
                m = dve.tensor_tensor_scan(seen[:, t, :], mask[:, t, :], zeros[:, 0:J], 0.0, ALU.add, ALU.add)
            s(m)
            dve.tensor_copy(totals[:, :], seen[:, :, J - 1]).then_inc(totals_done, 1)
            dve.wait_ge(before_mm, 1)
            s(dve.tensor_scalar(before[:, :], before_p, -1.0, None, ALU.add))
            for t in range(NT):
                m = dve.scalar_tensor_tensor(mask[:, t, :], seen[:, t, :], before[:, t:t + 1], mask[:, t, :], ALU.add, ALU.mult)
            s(m)
            s(dve.tensor_reduce(rank[:, :], mask[:, :, :].rearrange("p t j -> p j t"), AX.X, ALU.add))
            s(dve.scalar_tensor_tensor(over_w[:, :], rank[:, :], float(CAP), rec[:, :, 1], ALU.is_ge, ALU.mult))
            s(dve.tensor_copy(tile_i[:, :], rank[:, :]))
            s(dve.tensor_scalar(src_i[:, :], tile_i[:, :], 7, None, ALU.logical_shift_right))
            s(dve.tensor_scalar(tile_i[:, :], tile_i[:, :], P - 1, None, ALU.bitwise_and))
            s(dve.scalar_tensor_tensor(tile_f[:, :], tile_f[:, :], float(C), src_i[:, :], ALU.mult, ALU.add))
            s(dve.scalar_tensor_tensor(tile_f[:, :], tile_i[:, :], float(NB), tile_f[:, :], ALU.mult, ALU.add))
            s(dve.tensor_scalar(rank[:, :], rank[:, :], float(CAP), float(2 * P * NB), ALU.is_ge, ALU.mult))
            dve.tensor_tensor(rec[:, :, 3].bitcast(I32), tile_f[:, :], rank[:, :], ALU.add).then_inc(records_set, 1)
            done = s.n

            dve.wait_ge(small_in, SMALL)
            dve.wait_ge(kv_added, KD)
            S1 = 2 + RSQRT_STEPS + 1

            def sweep1(t, b, k):
                s = Steps(dve, dve_step, done + t * S1)
                dve.wait_ge(x_loaded[b], 16 * k)
                s(dve.bn_stats(stat1[0:T, :], x_in[0:T, b, :]), dve_passed)
                s(dve.bn_aggr(mv1[0:T, :], stat1[0:T, :]))
                s(dve.tensor_scalar(rs1[0:T, 0:1], mv1[0:T, 1:2], EPS, None, ALU.add))
                rsqrt(dve, s, rs1[0:T, 0:1], rs1[0:T, 1:2], rs1[0:T, 2:3])
                assert s.n == S1
                if not isinstance(t, int) or t:
                    dve.wait_ge(xn_turned, t)
                dve.tensor_scalar(xn[0:T, :], x_in[0:T, b, :], mv1[0:T, 0:1], rs1[0:T, 1:2], ALU.subtract, ALU.mult).then_inc(x_normed, 1)
                dve.wait_ge(proj_done, t + 1)
                dve.wait_ge(q_exped, KD * (t + 1))
                dve.tensor_tensor(k_z[0:T, :], k_p[0:T, :], bk_s[0:T, :], ALU.add).then_inc(k_zed, 1)
                dve.wait_ge(kv_added, KD + t)
                dve.tensor_tensor(v_one[0:T, :, 0:P], v_p[0:T, :].rearrange("p (c n) -> p c n", c=KD),
                                  bv_s[0:T, :].rearrange("p (c n) -> p c n", c=KD), ALU.add).then_inc(v_set, 1)
                for c in range(KD):
                    m = dve.tensor_scalar(q_pos[:, c, :], q_p[:, c, :], bq_s[:, c:c + 1], 0.0, ALU.add, ALU.max)
                m.then_inc(q_pos_set, 1)
                dve.wait_ge(q_pos_set, t + 1)
                dve.scalar_tensor_tensor(q_t[:, :, bass.ds(t * T, T)], q_exp[:, :, :], 1.0, q_pos[:, :, :], ALU.min, ALU.add).then_inc(q_set, 1)
                dve.wait_ge(k_exped, t + 1)
                dve.tensor_scalar(k_z[0:T, :], k_z[0:T, :], 0.0, None, ALU.max).then_inc(k_pos_set, 1)
                dve.wait_ge(k_pos_set, t + 1)
                dve.scalar_tensor_tensor(k_map[0:T, :], k_exp[0:T, :], 1.0, k_z[0:T, :], ALU.min, ALU.add).then_inc(k_set, 1)

            sweep1(0, 0, 1)
            with dve.Fori(0, (NT - 1) // 2) as i:
                sweep1(2 * i + 1, 1, i + 1)
                sweep1(2 * i + 2, 0, i + 2)
            done = done + NT * S1

            dve.wait_ge(kv_added, KD + NT)
            dve.memset(k_map[:, :], 0.0).then_inc(kv_ready, 1)
            dve.wait_ge(kv_total, 1)
            for c in range(KD):
                for g in range(P // HD):
                    r = slice(g * HD, (g + 1) * HD)
                    dve.tensor_copy(kv_s[r, c, r], kv_p[c][r, r])
                    m = dve.tensor_copy(kv_s[r, c, P + g:P + g + 1], kv_p[c][r, P:P + 1])
            m.then_inc(kv_ready, 1)

            with dve.Fori(0, NE) as e:
                for i, (wh, wl) in enumerate(((w1h, w1l), (w2h, w2l))):
                    dve.wait_ge(split_high, 2 * e + i + 1)
                    dve.tensor_tensor(wl[:, bass.ds(e, 1), :, :].rearrange("p e k n -> p (e k n)"), stage[:, i, :],
                                      wh[:, bass.ds(e, 1), :, :].rearrange("p e k n -> p (e k n)").bitcast(F32),
                                      ALU.subtract).then_inc(split_low, 1)
            dve.wait_ge(wr_split, 1)
            dve.tensor_tensor(wr_l[:, :, :], wr_s[:, :, :], wr_h[:, :, :].bitcast(F32), ALU.subtract).then_inc(wr_split, 1)

            S2 = 3

            def sweep2(t, b, k):
                s = Steps(dve, dve_step, done + t * S2)
                dve.wait_ge(attn_mm, t + 1)
                s(dve.tensor_scalar(norm[0:T, :].rearrange("p (c g) -> p c g", c=KD), attn_p[0:T, :, P:NK], 1e-6, None, ALU.add))
                s(dve.reciprocal(norm[0:T, :], norm[0:T, :]))
                for c in range(KD):
                    g = P // HD
                    m = dve.tensor_tensor(attn[0:T, c * P:(c + 1) * P].rearrange("p (g d) -> p g d", g=g),
                                          attn_p[0:T, c, 0:P].rearrange("p (g d) -> p g d", g=g),
                                          norm[0:T, c * g:(c + 1) * g].unsqueeze(2).to_broadcast([T, g, HD]), ALU.mult)
                m.then_inc(attn_set, 1)
                dve.wait_ge(x_loaded[b], 16 * k)
                s(dve.tensor_tensor(x_in[0:T, b, :], x_in[0:T, b, :], bo_s[0:T, :], ALU.add))
                assert s.n == S2
                dve.wait_ge(mix_mm, t + 1)
                if not isinstance(t, int) or t:
                    dve.wait_ge(mix_stored, 16 * t)
                dve.tensor_tensor(mix_out[0:T, :], mix_p[0:T, :], x_in[0:T, b, :], ALU.add).then_inc(mix_set, 1)

            sweep2(0, 1, NT // 2 + 1)
            with dve.Fori(0, (NT - 1) // 2) as i:
                sweep2(2 * i + 1, 0, NT // 2 + 1 + i + 1)
                sweep2(2 * i + 2, 1, NT // 2 + 1 + i + 1)
            done = done + NT * S2
            dve.wait_ge(mix_stored, 16 * NT)
            dve.wait_ge(chunk_out[0], 16 * C * (CH // 2 + 1))
            dve.wait_ge(chunk_out[1], 16 * C * (CH // 2))
            dve.memset(mv[:, :, :], 0.0).then_inc(stage2_done, 1)

            def one_hot(t, b, c, k):
                if c == 0:
                    dve.wait_ge(slots_in[b], 16 * (k + 1))
                if not isinstance(t, int) or t:
                    dve.wait_ge(block_added, (t - 1) * C + c + 1)
                dve.tensor_scalar(onehot[:, c, :], iota_row[:, :], slot_rec[:, b, c, 0:1], slot_rec[:, b, c, 1:2],
                                  ALU.is_equal, ALU.mult).then_inc(onehot_set, 1)

            def norms(p, tiles, s):
                dve.wait_ge(block_added, (2 * p + tiles) * C)
                for b in range(tiles):
                    t = 2 * p + b
                    dve.wait_ge(rest_in[b], 32 * (p + 1))
                    s(dve.tensor_tensor(z[0:T, b, :], agg[0:T, b, :], extra_in[0:T, b, :], ALU.add))
                    dve.scalar_tensor_tensor(x2[0:T, b, :], z[0:T, b, :], 0.0, mixed_in[0:T, b, :], ALU.max, ALU.add).then_inc(x2_set, 1)
                    dve.wait_ge(x2_set, t + 1)
                for now in (x2, z):
                    for b in range(tiles):
                        m = dve.bn_stats(stat[0:T, b, :], now[0:T, b, :])
                    s(m, dve_passed)
                    for b in range(tiles):
                        m = dve.bn_aggr(mv[0:T, b, :], stat[0:T, b, :])
                    s(m)
                    s(dve.tensor_scalar(rs[0:T, 0, :], mv[0:T, :, 1], EPS, None, ALU.add))
                    rsqrt(dve, s, rs[0:T, 0, :], rs[0:T, 1, :], rs[0:T, 2, :])
                    if now is x2:
                        for b in range(tiles):
                            m = dve.tensor_scalar(z[0:T, b, :], x2[0:T, b, :], mv[0:T, b, 0:1], rs[0:T, 1, b:b + 1],
                                                  ALU.subtract, ALU.mult)
                        s(m)
                for b in range(tiles):
                    m = dve.scalar_tensor_tensor(z[0:T, b, :], z[0:T, b, :], mv[0:T, b, 0:1], gamma_s[0:T, :], ALU.subtract, ALU.mult)
                s(m)
                for b in range(tiles):
                    m = dve.scalar_tensor_tensor(z[0:T, b, :], z[0:T, b, :], rs[0:T, 1, b:b + 1], beta_s[0:T, :], ALU.mult, ALU.add)
                m.then_inc(normed, 1)

            def norm_steps(tiles):
                return tiles + 2 * (3 + RSQRT_STEPS) + 2

            def low_halves(p):
                dve.wait_ge(xf_high, p + 1)
                dve.tensor_tensor(xf_l[:, :, :].rearrange("p k n -> p (k n)"), misc[:, 0:KD * W2T],
                                  xf_h[:, :, :].rearrange("p k n -> p (k n)").bitcast(F32), ALU.subtract).then_inc(xf_low, 1)

            ROUTE = 10

            def route(p, tiles, s):
                n0 = s.n
                dve.wait_ge(logits_mm, p + 1)
                s(dve.tensor_tensor(logit[0:T, 0:tiles, :], misc[0:T, 0:tiles * NE].rearrange("p (b e) -> p b e", b=tiles),
                                    br_s[0:T, :].unsqueeze(1).to_broadcast([T, tiles, NE]), ALU.add), dve_passed)
                for b in range(tiles):
                    m = dve.max(top[0:T, b, :], logit[0:T, b, :])
                s(m)
                dve.tensor_tensor(share[0:T, 0:tiles, 0:1], top[0:T, 0:tiles, 0:1], top[0:T, 0:tiles, 1:2],
                                  ALU.subtract).then_inc(diff_set, 1)
                for b in range(tiles):
                    m = dve.max_index(top_at[0:T, b, :], top[0:T, b, :], logit[0:T, b, :])
                s(m)
                s(dve.tensor_copy(top_f[0:T, 0:tiles, 0:2], top_at[0:T, 0:tiles, 0:2]))
                dve.wait_ge(tanh_set, p + 1)
                dve.tensor_scalar(share[0:T, 0:tiles, 2:3], share[0:T, 0:tiles, 1:2], 0.5, 0.5, ALU.mult, ALU.add)
                s(dve.tensor_scalar(share[0:T, 0:tiles, 3:4], share[0:T, 0:tiles, 1:2], -0.5, 0.5, ALU.mult, ALU.add))
                for b in range(tiles):
                    m = dve.tensor_scalar(gate[0:T, b, :], iota_row[0:T, 0:NE], top_f[0:T, b, 0:1], share[0:T, b, 2:3],
                                          ALU.is_equal, ALU.mult)
                s(m)
                for b in range(tiles):
                    m = dve.tensor_scalar(logit[0:T, b, :], iota_row[0:T, 0:NE], top_f[0:T, b, 1:2], share[0:T, b, 3:4],
                                          ALU.is_equal, ALU.mult)
                s(m)
                dve.tensor_tensor(gate[0:T, 0:tiles, :], gate[0:T, 0:tiles, :], logit[0:T, 0:tiles, :], ALU.add).then_inc(gate_set, 1)
                dve.wait_ge(gate_set, p + 1)
                assert s.n - n0 == ROUTE_STEPS

            ROUTE_STEPS = 7

            def split(p, e, n):
                x_ = p * NE + e
                dve.wait_ge(h_set, HC * (x_ + 1))
                if e >= 2:
                    dve.wait_ge(expert_mm, x_ - 1)
                dve.tensor_copy(h_h[:, e % 2, :, 0:n], h[:, :, 0:n]).then_inc(h_high, 1)
                dve.wait_ge(h_high, x_ + 1)
                dve.tensor_tensor(h_l[:, e % 2, :, 0:n], h[:, :, 0:n], h_h[:, e % 2, :, 0:n].bitcast(F32), ALU.subtract).then_inc(h_split, 1)

            def begin_y(p, tiles):
                dve.wait_ge(bias_mm, p + 1)
                if not isinstance(p, int) or p:
                    dve.wait_ge(y_stored, 16 * 2 * p)
                dve.tensor_tensor(y[0:T, 0:tiles, :], misc[0:T, 0:tiles * D].rearrange("p (b n) -> p b n", b=tiles),
                                  x2[0:T, 0:tiles, :], ALU.add).then_inc(y_begun, 1)
                dve.wait_ge(y_begun, p + 1)

            def add_y(p, e, tiles):
                x_ = p * NE + e
                dve.wait_ge(expert_mm, x_ + 1)
                for b in range(tiles):
                    m = dve.scalar_tensor_tensor(y[0:T, b, :], yp[0:T, e % 2, b, :], gate[0:T, b, e:e + 1], y[0:T, b, :],
                                                 ALU.mult, ALU.add)
                m.then_inc(y_added, 1)
                dve.wait_ge(y_added, x_ + 1)

            def pair(p, tiles, nxt, s):
                n = W2T if tiles == 2 else T + 1
                todo = [(b, c) for b in range(nxt) for c in range(C)]
                part = -(-len(todo) // 6)
                for e in range(NE):
                    for b, c in todo[e * part:(e + 1) * part]:
                        one_hot(2 * p + 2 + b, b, c, p + 1)
                    if e == 0:
                        route(p, tiles, s)
                    if e == 7 and nxt:
                        add_y(p, e - 1, tiles)
                        norms(p + 1, nxt, s)
                        split(p, e, n)
                        continue
                    split(p, e, n)
                    if e == 1:
                        begin_y(p, tiles)
                    if e:
                        add_y(p, e - 1, tiles)
                add_y(p, NE - 1, tiles)
                if nxt:
                    low_halves(p + 1)

            s = Steps(dve, dve_step, done)
            for b in range(2):
                for c in range(C):
                    one_hot(b, b, c, 0)
            norms(0, 2, s)
            low_halves(0)
            done = done + s.n
            PER = ROUTE_STEPS + norm_steps(2)
            with dve.Fori(0, PAIRS - 1) as p:
                s = Steps(dve, dve_step, done + p * PER)
                pair(p, 2, 2, s)
                assert s.n == PER, s.n
            done = done + (PAIRS - 1) * PER
            s = Steps(dve, dve_step, done)
            pair(PAIRS - 1, 2, 1, s)
            pair(PAIRS, 1, 0, s)


_INS = ["x", "src", "dst", "edge_weight", "L0_gnn_weight", "L0_mix_wq", "L0_mix_bq", "L0_mix_wk", "L0_mix_bk",
        "L0_mix_wv", "L0_mix_bv", "L0_mix_wo", "L0_mix_bo", "L0_ffn_gamma", "L0_ffn_beta", "L0_ffn_Wr",
        "L0_ffn_br", "L0_ffn_W1", "L0_ffn_b1", "L0_ffn_W2", "L0_ffn_b2"]


def kernel(**inputs):
    import numpy as _np
    import concourse.bacc as _bacc
    from concourse import mybir as _mybir
    from concourse.bass_utils import run_bass_kernel_spmd as _run

    nc = _bacc.Bacc("TRN2", target_bir_lowering=False, num_devices=1)
    arrays, args = {}, []
    for name in _INS:
        a = _np.ascontiguousarray(inputs[name])
        arrays[f"in_{name}"] = a
        args.append(nc.dram_tensor(f"in_{name}", a.shape, _mybir.dt.from_np(a.dtype), kind="ExternalInput").ap())
    args.append(nc.dram_tensor("out_0", (N, D), F32, kind="ExternalOutput").ap())
    build(nc, *args)
    r = _run(nc, [arrays], core_ids=[0])
    return r.results[0]["out_0"]
```

```python
from contextlib import ExitStack

import concourse.bass as bass
from concourse import mybir

F32, F32R, I32, U32 = mybir.dt.float32, mybir.dt.float32r, mybir.dt.int32, mybir.dt.uint32
ALU = mybir.AluOpType
ACT = mybir.ActivationFunctionType
AX = mybir.AxisListType

P = 128
N, D = 3125, 256
T = 125
NT = N // T
E = 50000
J = -(-E // P)
LAST = E - (P - 1) * J
C = 17
CAP = C * P
NB = NT * C
CH = J // C
HEADS, HD = 8, 32
NE, HID = 8, 512
HC = HID // P
KD = D // P
W2T = 2 * T
PAIRS = NT // 2
SUM_EXPERTS = 4
PART = -(-2 * C // SUM_EXPERTS)
NORM_FROM = 3
HIGH = PART
EPS = 1e-5
RSQRT_BITS = 0x5F3759DF
assert CH * C == J and CH % 2 == 1 and NT % 2 == 1 and NT * T == N


def apart(eng, passed):
    eng.sem_inc(passed, 1)


def has(t):
    return not isinstance(t, int) or 0 <= t < NT


def over_tiles(eng, first, lo, hi, last, step):
    for t in range(first, lo):
        step(t, t % 2)
    with eng.Fori(lo // 2, hi // 2) as i:
        step(2 * i, 0)
        step(2 * i + 1, 1)
    for t in range(hi, last):
        step(t, t % 2)


class Steps:

    def __init__(self, eng, sem, before=0):
        self.eng, self.sem, self.before, self.n = eng, sem, before, 0

    def __call__(self, ins, passed=None):
        self.n += 1
        ins.then_inc(self.sem, 1)
        self.eng.wait_ge(self.sem, self.before + self.n)
        if passed is not None:
            apart(self.eng, passed)


def rsqrt(eng, s, v, y, a):
    s(eng.tensor_scalar(y.bitcast(I32), v.bitcast(I32), 1, None, ALU.logical_shift_right))
    s(eng.tensor_scalar(y.bitcast(I32), y.bitcast(I32), -1.0, float(RSQRT_BITS), ALU.mult, ALU.add))
    for _ in range(3):
        s(eng.scalar_tensor_tensor(a, y, -0.5, y, ALU.mult, ALU.mult))
        s(eng.tensor_tensor(a, a, v, ALU.mult))
        s(eng.scalar_tensor_tensor(y, a, 1.5, y, ALU.add, ALU.mult))


RSQRT_STEPS = 11


def build(nc, x, src, dst, edge_weight, w_gnn, wq, bq, wk, bk, wv, bv, wo, bo, gamma, beta, Wr, br,
          W1, b1, W2, b2, out):
    ctx = ExitStack()
    with ctx:
        def sb(name, shape, dt=F32, where=ctx):
            return where.enter_context(nc.sbuf_tensor(name, shape, dt))

        def sem(name):
            return ctx.enter_context(nc.semaphore(name))

        slots = nc.dram_tensor("slots", (P * NB, 4), F32, kind="Internal").ap()
        slots_by_lane = slots.rearrange("(p b) r -> p b r", p=P)
        table = nc.dram_tensor("table", (N, D), F32, kind="Internal").ap()
        mixed = nc.dram_tensor("mixed", (N, D), F32, kind="Internal").ap()
        extra = nc.dram_tensor("extra", (N, D), F32, kind="Internal").ap()

        iota_row = sb("iota_row", [P, T])
        ident = sb("ident", [P, P])
        over_n = sb("over_n", [P, 1])
        over_any = sb("over_any", [1, 1], I32)
        ones = sb("ones", [P, 1])

        with ExitStack() as early:
            src_i = sb("src_i", [P, J], I32, early)
            dst_i = sb("dst_i", [P, J], I32, early)
            weight = sb("weight", [P, J], F32, early)
            tile_i = sb("tile_i", [P, J], I32, early)
            tile_f = sb("tile_f", [P, J], F32, early)
            rest = sb("rest", [P, J], F32, early)
            zeros = sb("zeros", [P, 1700], F32, early)
            mask = sb("mask", [P, NT, J], F32, early)
            seen = sb("seen", [P, NT, J], F32, early)
            rank = sb("rank", [P, J], F32, early)
            above = sb("above", [P, P], F32, early)
            totals = sb("totals", [P, NT], F32, early)
            before = sb("before", [P, NT], F32, early)
        w1h = sb("w1h", [P, NE, KD, HID], F32R)
        w1l = sb("w1l", [P, NE, KD, HID], F32R)
        w2h = sb("w2h", [P, NE, HC, D], F32R)
        w2l = sb("w2l", [P, NE, HC, D], F32R)

        gamma_s, beta_s = sb("gamma_s", [P, D]), sb("beta_s", [P, D])
        br_s = sb("br_s", [P, NE])
        b1_s = sb("b1_s", [P, NE, HC])
        b2_s = sb("b2_s", [NE, D])
        wr_s = sb("wr_s", [P, KD, NE])
        wr_h = sb("wr_h", [P, KD, NE], F32R)
        wr_l = sb("wr_l", [P, KD, NE], F32R)

        edges = ExitStack()
        rec = sb("rec", [P, J, 4], F32, edges)
        over_w = sb("over_w", [P, J], F32, edges)
        row_now = sb("row_now", [P, 1], F32, edges)
        col_now = sb("col_now", [P, 1], I32, edges)
        src_f = sb("src_f", [P, J], F32, edges)
        with ExitStack() as mid:
            q_t = sb("q_t", [P, KD, N], F32, mid)
            wq_s, wk_s, wv_s, wo_s, wg_s = (sb(n, [P, KD, D], F32, mid)
                                            for n in ("wq_s", "wk_s", "wv_s", "wo_s", "wg_s"))
            bk_s, bv_s, bo_s = (sb(n, [P, D], F32, mid) for n in ("bk_s", "bv_s", "bo_s"))
            bq_s = sb("bq_s", [P, KD], F32, mid)
            x_in = sb("x_in", [P, 2, D], F32, mid)
            xn = sb("xn", [P, 2, D], F32, mid)
            xn_t = sb("xn_t", [P, 2, KD, T], F32, mid)
            stat1 = sb("stat1", [P, 6], F32, mid)
            mv1 = sb("mv1", [P, 2], F32, mid)
            rs1 = sb("rs1", [P, 4], F32, mid)
            q_exp = sb("q_exp", [P, KD, T], F32, mid)
            q_pos = sb("q_pos", [P, KD, T], F32, mid)
            k_z = sb("k_z", [P, D], F32, mid)
            k_exp = sb("k_exp", [P, D], F32, mid)
            k_map = sb("k_map", [P, 2, D], F32, mid)
            v_one = sb("v_one", [P, 2, KD, P + 1], F32, mid)
            g_out = sb("g_out", [P, D], F32, mid)
            kv_s = sb("kv_s", [P, KD, P + HEADS // KD], F32, mid)
            q_now = xn_t
            norm = sb("norm", [P, HEADS], F32, mid)
            attn = xn
            attn_t = sb("attn_t", [P, 2, KD, T], F32, mid)
            mix_out = k_map
            rec_buf = sb("rec_buf", [P, 2, C, 4], F32, mid)
            stage = sb("stage", [P, 2, NE // 4 * D * 2], F32, mid)
        with ExitStack() as between:
            over_acc = sb("over_acc", [P, NT, D], F32, between)
            over_rows = sb("over_rows", [P, D], F32, between)
            hot_now = sb("hot_now", [P, T], F32, between)
        edges.close()
        rows = sb("rows", [P, C, D], F32R)
        rows_h = sb("rows_h", [P, HIGH, D], F32R)
        onehot = sb("onehot", [P, 2, PART, T], F32R)
        slot_rec = sb("slot_rec", [P, 2, C, 4])
        mixed_in = sb("mixed_in", [P, 2, D])
        extra_in = sb("extra_in", [P, 2, D])
        x2 = sb("x2", [P, 2, D])
        z = sb("z", [P, 2, D])
        stat = sb("stat", [P, 2, 6])
        mv = sb("mv", [P, 2, 2])
        rs = sb("rs", [P, 3, 2])
        xf_h = sb("xf_h", [P, KD, W2T], F32R)
        xf_l = sb("xf_l", [P, KD, W2T], F32R)
        h = sb("h", [P, HC, W2T])
        h_h = sb("h_h", [P, 2, HC, W2T], F32R)
        h_l = sb("h_l", [P, 2, HC, W2T], F32R)
        logit = sb("logit", [P, 2, NE])
        top = sb("top", [P, 2, NE])
        top_at = sb("top_at", [P, 2, NE], U32)
        top_f = sb("top_f", [P, 2, NE])
        share = sb("share", [P, 2, 4])
        gate = sb("gate", [P, 2, NE])
        gate_t = sb("gate_t", [NE, 2, T])
        y = sb("y", [P, 2, D])
        hp = ctx.enter_context(nc.psum_tensor("hp", [P, 2, HC, 256], F32))
        yp = ctx.enter_context(nc.psum_tensor("yp", [P, 2, 2, D], F32))
        agg = ctx.enter_context(nc.psum_tensor("agg", [P, 2, D], F32))
        misc = ctx.enter_context(nc.psum_tensor("misc", [P, 512], F32))
        banks = hp[:, :, :, :].rearrange("p a (b c) n -> p (a b) (c n)", b=2)
        q_p = [b[:, 0:W2T].rearrange("p (c n) -> p c n", c=KD) for b in (banks[:, 0, :], misc[:, :])]
        kv_now = [banks[:, 1, :], agg[:, :, :].rearrange("p a n -> p (a n)")]
        k_p, v_p = [b[:, 0:D] for b in kv_now], [b[:, D:2 * D] for b in kv_now]
        g_p = banks[:, 2, 0:D]
        mix_p = banks[:, 2, 0:D]
        xn_tp = banks[:, 3, 0:W2T].rearrange("p (c n) -> p c n", c=KD)
        over_p = misc[0:1, 0:1]
        before_p = banks[:, 3, 0:NT]
        NK = P + HEADS // KD
        attn_p = [banks[:, b, 0:KD * NK].rearrange("p (c n) -> p c n", c=KD) for b in range(2)]
        kv_p = [yp[:, c, :, :].rearrange("p a n -> p (a n)")[:, 0:P + 1] for c in range(KD)]

        (pads_set, edges_in, zeros_set, zeros_out, consts_set, totals_done, before_mm, records_set,
         dve_step) = map(sem, ("pads_set", "edges_in", "zeros_set", "zeros_out", "consts_set",
                               "totals_done", "before_mm", "records_set", "dve_step"))
        chunk_in = [sem(f"chunk_in{i}") for i in range(2)]
        chunk_out = [sem(f"chunk_out{i}") for i in range(2)]
        (small_in, x_loaded0, x_loaded1, x_normed, xn_turned, xn_t_set, proj_done, q_exped, k_zed,
         k_exped, k_set, v_set, q_set, g_copied, g_stored, kv_added) = map(sem, (
             "small_in", "x_loaded0", "x_loaded1", "x_normed", "xn_turned", "xn_t_set", "proj_done",
             "q_exped", "k_zed", "k_exped", "k_set", "v_set", "q_set", "g_copied", "g_stored",
             "kv_added"))
        x_loaded = [x_loaded0, x_loaded1]
        kv_total, kv_ready, split_in0, split_in1, split_high, split_low = map(sem, (
            "kv_total", "kv_ready", "split_in0", "split_in1", "split_high", "split_low"))
        split_in = [split_in0, split_in1]
        q_copied, attn_mm, attn_set, attn_turned, attn_t_set, mix_mm, mix_set = map(
            sem, ("q_copied", "attn_mm", "attn_set", "attn_turned", "attn_t_set", "mix_mm",
                  "mix_set"))
        mix_stored = [sem(f"mix_stored{i}") for i in range(2)]
        slots_in = [sem(f"slots_in{i}") for i in range(2)]
        rest_in = [sem(f"rest_in{i}") for i in range(2)]
        row_in = [sem(f"row_in{c}") for c in range(C)]
        onehot_set, block_added, x2_set, normed, turned, xf_high, xf_low = map(sem, (
            "onehot_set", "block_added", "x2_set", "normed", "turned", "xf_high",
            "xf_low"))
        (logits_mm, diff_set, tanh_set, gate_set, gate_turned, gate_copied, bias_mm, y_begun,
         hidden_mm, h_set, h_high, h_split, expert_mm, y_added, y_stored) = map(sem, (
             "logits_mm", "diff_set", "tanh_set", "gate_set", "gate_turned", "gate_copied",
             "bias_mm", "y_begun", "hidden_mm", "h_set", "h_high", "h_split", "expert_mm",
             "y_added", "y_stored"))
        stage2_done = sem("stage2_done")
        over_counted, over_mm, over_set = sem("over_counted"), sem("over_mm"), sem("over_set")
        (over_col, over_row, over_hot, over_sum, over_added, over_row_set, over_stored, over_step) = map(sem, (
            "over_col", "over_row", "over_hot", "over_sum", "over_added", "over_row_set", "over_stored",
            "over_step"))
        norm_set, x_biased = sem("norm_set"), sem("x_biased")
        pool_passed, dve_passed, pe_passed = sem("pool_passed"), sem("dve_passed"), sem("pe_passed")
        q_pos_set, k_pos_set = sem("q_pos_set"), sem("k_pos_set")
        wr_split = sem("wr_split")
        rows_high, rows_low = sem("rows_high"), sem("rows_low")

        def part_of(nxt, e):
            return [(b, c) for b in range(nxt) for c in range(C)][e * PART:(e + 1) * PART], e * PART

        block = ctx.enter_context(nc.Block())
        SMALL = 16 * 15

        def when_over(eng):
            eng.wait_ge(over_set, 1)
            return eng.If(eng.value_load(over_any[0:1, 0:1], min_val=0, max_val=1) > 0)

        def over_pool(pool):
            with when_over(pool):
                with pool.Fori(0, J) as j:
                    pool.wait_ge(over_col, j + 1)
                    apart(pool, pool_passed)
                    pool.indirect_dma_start(over_rows[:, :], None, table,
                                            bass.IndirectOffsetOnAxis(ap=col_now[:, 0:1], axis=0)).then_inc(over_row, 16)

        def over_pe(pe):
            with when_over(pe):
                with pe.Fori(0, J) as j:
                    pe.wait_ge(over_row, 16 * (j + 1))
                    apart(pe, pe_passed)
                    with pe.Fori(0, NT) as t:
                        pe.wait_ge(over_hot, j * NT + t + 1)
                        pe.matmul(agg[0:T, 0, :], hot_now[:, :], over_rows[:, :], start=True, stop=True).then_inc(over_sum, 1)

        def over_sp(sp):
            with when_over(sp):
                sp.wait_ge(over_added, NT * J + 1)
                sp.dma_start(extra.rearrange("(t p) n -> p t n", p=T), over_acc[0:T, :, :]).then_inc(over_stored, 16)
                sp.wait_ge(over_stored, 16)

        def over_dve(dve):
            with when_over(dve):
                dve.memset(over_acc[:, :, :], 0.0).then_inc(over_added, 1)
                dve.wait_ge(over_added, 1)
                with dve.Fori(0, J) as j:
                    dve.tensor_copy(col_now[:, :], rec[:, bass.ds(j, 1), 2].bitcast(I32)).then_inc(over_col, 1)
                    dve.tensor_copy(row_now[:, :], src_f[:, bass.ds(j, 1)]).then_inc(over_row_set, 1)
                    dve.wait_ge(over_row_set, j + 1)
                    apart(dve, dve_passed)
                    with dve.Fori(0, NT) as t:
                        q = j * NT + t
                        dve.tensor_scalar(hot_now[:, :], iota_row[:, :], row_now[:, 0:1], over_w[:, bass.ds(j, 1)],
                                          ALU.is_equal, ALU.mult).then_inc(over_hot, 1)
                        dve.wait_ge(over_hot, q + 1)
                        dve.tensor_scalar(row_now[:, :], row_now[:, :], -float(T), None, ALU.add).then_inc(over_step, 1)
                        dve.wait_ge(over_step, q + 1)
                        dve.wait_ge(over_sum, q + 1)
                        dve.tensor_tensor(over_acc[0:T, bass.ds(t, 1), :], over_acc[0:T, bass.ds(t, 1), :],
                                          agg[0:T, 0:1, :], ALU.add).then_inc(over_added, 1)
                        dve.wait_ge(over_added, q + 2)
                        apart(dve, dve_passed)
                dve.wait_ge(over_stored, 16)

        def by_chunk(w):
            return w.rearrange("(k p) n -> p k n", p=P)

        def to_rows(b):
            return b.rearrange("(a n) -> a n", a=1).to_broadcast([P, b.shape[0]])

        @block.sync
        def _(sp):
            sp.wait_ge(pads_set, 3)
            for t, v in ((src_i, src), (dst_i, dst), (weight, edge_weight)):
                sp.dma_start(t[0:P - 1, :], v[0:(P - 1) * J].rearrange("(p j) -> p j", p=P - 1)).then_inc(edges_in, 16)
                sp.dma_start(t[P - 1:P, 0:LAST], v[(P - 1) * J:E].rearrange("(p j) -> p j", p=1)).then_inc(edges_in, 16)
            sp.wait_ge(zeros_set, 1)
            sp.dma_start(slots_by_lane.rearrange("p b r -> p (b r)"), zeros[:, 0:NB * 4]).then_inc(zeros_out, 16)
            for i in range(4):
                w = N * D // T // 4
                sp.dma_start(extra.rearrange("(p a) n -> p (a n)", p=T)[:, i * w:(i + 1) * w],
                             zeros[0:T, 0:w]).then_inc(zeros_out, 16)

            def chunk(c, b, k):
                sp.dma_start(rec_buf[:, b, :, :].rearrange("p c r -> p (c r)"),
                             rec[:, bass.ds(c * C, C), :].rearrange("p c r -> p (c r)"))\
                    .then_inc(chunk_in[b], 16)

            sp.wait_ge(records_set, 1)
            chunk(0, 0, 0)
            chunk(1, 1, 0)
            with sp.Fori(1, CH // 2) as i:
                for b in range(2):
                    sp.wait_ge(chunk_out[b], 16 * C * i)
                    chunk(2 * i + b, b, i)
            sp.wait_ge(chunk_out[0], 16 * C * (CH // 2))
            chunk(CH - 1, 0, CH // 2)

            sp.wait_ge(chunk_out[0], 16 * C * (CH // 2 + 1))
            sp.wait_ge(chunk_out[1], 16 * C * (CH // 2))
            sp.wait_ge(zeros_out, 16 * 5)
            sp.wait_ge(mix_stored[0], 16 * (NT // 2))
            sp.wait_ge(mix_stored[1], 16 * (NT // 2 + 1))
            sp.wait_ge(g_stored, 16 * NT)

            sp.wait_ge(stage2_done, 1)
            over_sp(sp)

            def load(t, b, k, first=False):
                if not first:
                    sp.wait_ge(block_added, (t - 1) * C)
                sp.dma_start(slot_rec[:, b, :, :].rearrange("p c r -> p (c r)"),
                             slots_by_lane[:, bass.ds(t * C, C), :].rearrange("p c r -> p (c r)"))\
                    .then_inc(slots_in[b], 16)
                if not first:
                    sp.wait_ge(x2_set, t - 1)
                sp.dma_start(mixed_in[0:T, b, :], mixed[bass.ds(t * T, T), :]).then_inc(rest_in[b], 16)
                sp.dma_start(extra_in[0:T, b, :], extra[bass.ds(t * T, T), :]).then_inc(rest_in[b], 16)

            def store(p, b):
                sp.dma_start(out[bass.ds((2 * p + b) * T, T), :], y[0:T, b, :]).then_inc(y_stored, 16)

            for t in range(4):
                load(t, t % 2, t // 2, t < 2)
            with sp.Fori(0, PAIRS - 2) as p:
                for b in range(2):
                    load(2 * p + 4 + b, b, p + 2)
                sp.wait_ge(y_added, NE * (p + 1))
                for b in range(2):
                    store(p, b)
            load(NT - 1, 0, PAIRS)
            for p in range(PAIRS - 2, PAIRS):
                sp.wait_ge(y_added, NE * (p + 1))
                for b in range(2):
                    store(p, b)
            sp.wait_ge(y_added, NE * (PAIRS + 1))
            store(PAIRS, 0)
            sp.wait_ge(y_stored, 16 * NT)

        @block.gpsimd
        def _(pool):
            pool.iota(iota_row[:, :], [[1, T]], base=0, channel_multiplier=0,
                      allow_small_or_imprecise_dtypes=True).then_inc(consts_set, 1)
            pool.memset(ident[:, :], 0.0).then_inc(consts_set, 1)
            pool.memset(above[:, :], 1.0).then_inc(consts_set, 1)
            pool.wait_ge(consts_set, 3)
            pool.affine_select(out=ident[:, :], in_=ident[:, :], compare_op=ALU.not_equal, fill=1.0,
                               base=0, pattern=[[-1, P]], channel_multiplier=1).then_inc(consts_set, 1)
            pool.affine_select(out=above[:, :], in_=above[:, :], compare_op=ALU.is_gt, fill=0.0,
                               base=0, pattern=[[1, P]], channel_multiplier=-1).then_inc(consts_set, 1)

            pool.wait_ge(zeros_out, 16 * 5)

            def scatter(b, k):
                pool.wait_ge(chunk_in[b], 16 * (k + 1))
                apart(pool, pool_passed)
                for c in range(C):
                    pool.indirect_dma_start(
                        slots, bass.IndirectOffsetOnAxis(ap=rec_buf[:, b, c, 3:4].bitcast(I32), axis=0),
                        rec_buf[:, b, c, :], None, bounds_check=P * NB - 1, oob_is_err=False)\
                        .then_inc(chunk_out[b], 16)

            with pool.Fori(0, CH // 2) as i:
                for b in range(2):
                    scatter(b, i)
            scatter(0, CH // 2)

            pool.wait_ge(stage2_done, 1)
            pool.wait_ge(g_stored, 16 * NT)

            over_pool(pool)

            def gather(t, b, k, first=False):
                pool.wait_ge(slots_in[b], 16 * (k + 1))
                apart(pool, pool_passed)
                for c in range(C):
                    if not first:
                        pool.wait_ge(block_added, (t - 1) * C + c + 1)
                        apart(pool, pool_passed)
                    pool.indirect_dma_start(
                        rows[:, c, :].bitcast(F32), None, table,
                        bass.IndirectOffsetOnAxis(ap=slot_rec[:, b, c, 2:3].bitcast(I32), axis=0))\
                        .then_inc(row_in[c], 16)

            gather(0, 0, 0, True)
            gather(1, 1, 0)
            with pool.Fori(1, PAIRS) as p:
                for b in range(2):
                    gather(2 * p + b, b, p)
            gather(NT - 1, 0, PAIRS)

        @block.scalar
        def _(act):
            for w, t in ((wq, wq_s), (wk, wk_s), (wv, wv_s), (wo, wo_s), (w_gnn, wg_s)):
                act.dma_start(t[:, :, :], by_chunk(w)).then_inc(small_in, 16)
            for b, t in ((bk, bk_s), (bv, bv_s), (bo, bo_s), (gamma, gamma_s), (beta, beta_s), (br, br_s)):
                act.dma_start(t[:, :], to_rows(b)).then_inc(small_in, 16)
            with nc.allow_non_contiguous_dma(reason="a few thousand numbers, once"):
                act.dma_start(bq_s[:, :], bq.rearrange("(k p) -> p k", p=P)).then_inc(small_in, 16)
                act.dma_start(b1_s[:, :, :], b1.rearrange("e (c p) -> p e c", p=P)).then_inc(small_in, 16)
            act.dma_start(b2_s[:, :], b2).then_inc(small_in, 16)
            act.dma_start(wr_s[:, :, :], by_chunk(Wr)).then_inc(small_in, 16)
            act.wait_ge(small_in, SMALL)

            def load_x(t, b):
                act.dma_start(x_in[0:T, b, :], x[bass.ds(t * T, T), :]).then_inc(x_loaded[b], 16)

            def sweep1(t, b):
                if has(t + 3):
                    act.wait_ge(x_normed, t + 2)
                    load_x(t + 3, 1 - b)
                if has(t + 1):
                    act.wait_ge(xn_turned, t + 2)
                    act.activation(xn_t[:, 1 - b, :, :], xn_tp, ACT.Copy).then_inc(xn_t_set, 1)
                act.wait_ge(proj_done, t + 1)
                if not isinstance(t, int) or t:
                    act.wait_ge(g_stored, 16 * t)
                    act.wait_ge(q_set, t)
                for c in range(KD):
                    act.activation(q_exp[:, c, :], q_p[b][:, c, :], ACT.Exp, bias=bq_s[:, c:c + 1]).then_inc(q_exped, 1)
                act.activation(g_out[0:T, :], g_p[0:T, :], ACT.Copy).then_inc(g_copied, 1)
                act.wait_ge(k_zed, t + 1)
                act.activation(k_exp[0:T, :], k_z[0:T, :], ACT.Exp).then_inc(k_exped, 1)
                act.wait_ge(g_copied, t + 1)
                act.dma_start(table[bass.ds(t * T, T), :], g_out[0:T, :]).then_inc(g_stored, 16)

            load_x(0, 0)
            load_x(1, 1)
            act.wait_ge(x_normed, 1)
            load_x(2, 0)
            act.wait_ge(xn_turned, 1)
            act.activation(xn_t[:, 0, :, :], xn_tp, ACT.Copy).then_inc(xn_t_set, 1)
            over_tiles(act, 0, 2, NT - 3, NT, sweep1)

            def stage_in(w, b):
                e = bass.ds(w, 1)
                act.dma_start(stage[:, b, :].rearrange("p (k n) -> p k n", k=(KD, HC)[b]),
                              (W1, W2)[b][e, :, :].rearrange("e (k p) n -> p (e k) n", p=P)).then_inc(split_in[b], 16)

            def sweep2(t, b, split=None):
                if has(t + 2):
                    if not isinstance(t, int) or t >= 0:
                        act.wait_ge(attn_mm, t + 1)
                    act.activation(q_now[:, b, :, :], q_t[:, :, bass.ds((t + 2) * T, T)], ACT.Copy).then_inc(q_copied, 1)
                if has(t):
                    act.wait_ge(attn_turned, t + 1)
                    if not isinstance(t, int) or t >= 2:
                        act.wait_ge(mix_mm, t - 1)
                    act.activation(attn_t[:, b, :, :], xn_tp, ACT.Copy).then_inc(attn_t_set, 1)
                if split is not None:
                    act.wait_ge(split_in[b], 16 * (split + 1))
                    act.activation((w1h, w2h)[b][:, bass.ds(split, 1), :, :].rearrange("p e k n -> p (e k n)"),
                                   stage[:, b, :], ACT.Copy).then_inc(split_high, 1)
                    if not (isinstance(split, int) and split == NE - 1):
                        act.wait_ge(split_low, 2 * split + b + 1)
                        stage_in(split + 1, b)
                if has(t - 1):
                    act.wait_ge(mix_set, t)
                    act.dma_start(mixed[bass.ds((t - 1) * T, T), :], mix_out[0:T, b, :]).then_inc(mix_stored[b], 16)
                if has(t + 1):
                    if not isinstance(t, int) or t >= 1:
                        act.wait_ge(mix_set, t)
                    load_x(t + 1, b)

            act.wait_ge(records_set, 1)
            act.wait_ge(zeros_out, 16 * 5)
            for b in range(2):
                stage_in(0, b)
            act.wait_ge(x_normed, NT)
            act.wait_ge(q_set, NT)
            sweep2(-2, 0)
            sweep2(-1, 1)
            for t in range(2):
                sweep2(t, t)
            with act.Fori(1, NE) as i:
                sweep2(2 * i, 0, i - 1)
                sweep2(2 * i + 1, 1, i - 1)
            for t in range(2 * NE, 2 * NE + 2):
                sweep2(t, t % 2, NE - 1)
            for t in range(2 * NE + 2, NT + 1):
                sweep2(t, t % 2)
            act.activation(wr_h[:, :, :], wr_s[:, :, :], ACT.Copy).then_inc(wr_split, 1)

            def halves(p):
                act.wait_ge(turned, p + 1)
                act.activation(xf_h[:, :, :].rearrange("p k n -> p (k n)"), misc[:, 0:KD * W2T], ACT.Copy).then_inc(xf_high, 1)

            def high_rows(p, nxt, e):
                blocks, first = part_of(nxt, e)
                for i, (b, c) in enumerate(blocks):
                    t, q = 2 * p + b, first + i
                    if q >= HIGH or not isinstance(p, int) or p:
                        act.wait_ge(block_added, 2 * p * C + max(q - HIGH + 1, 0))
                    act.wait_ge(row_in[c], 16 * (t + 1))
                    act.activation(rows_h[:, q % HIGH, :], rows[:, c, :].bitcast(F32), ACT.Copy,
                                   scale=slot_rec[:, b, c, 1:2]).then_inc(rows_high, 1)

            def expert(p, e, n):
                x_ = p * NE + e
                for c in range(HC):
                    if c % 2 == 0:
                        act.wait_ge(hidden_mm, 2 * x_ + c // 2 + 1)
                        if e or not isinstance(p, int) or p:
                            act.wait_ge(h_split, 2 * x_ + c // 2 - 1 if e or c else 2 * x_)
                    act.activation(h[:, c, 0:n], hp[:, e % 2, c, 0:n], ACT.Gelu,
                                   bias=b1_s[:, e, c:c + 1]).then_inc(h_set, 1)
                    if c % 2:
                        if c == 1 and (e >= 2 or not isinstance(p, int) or p):
                            act.wait_ge(expert_mm, x_ - 1 if e >= 2 else p * NE)
                        act.wait_ge(h_set, HC * x_ + c + 1)
                        act.activation(h_h[:, e % 2, c - 1:c + 1, 0:n], h[:, c - 1:c + 1, 0:n], ACT.Copy).then_inc(h_high, 1)

            def pair(p, tiles, nxt):
                for e in range(NE):
                    expert(p, e, W2T if tiles == 2 else T + 1)
                    if e == 0:
                        act.wait_ge(diff_set, p + 1)
                        act.activation(share[0:T, 0:tiles, 1:2], share[0:T, 0:tiles, 0:1], ACT.Tanh, scale=0.5).then_inc(tanh_set, 1)
                    if e == 1:
                        act.wait_ge(gate_turned, p + 1)
                        act.activation(gate_t[:, 0:tiles, :], misc[0:NE, 0:tiles * T].rearrange("p (b n) -> p b n", b=tiles), ACT.Copy).then_inc(gate_copied, 1)
                    high_rows(p + 1, nxt, e + 1)
                if nxt:
                    halves(p + 1)
                if nxt == 2:
                    high_rows(p + 2, 1, 0)

            for e in range(NE):
                high_rows(0, 2, e)
            halves(0)
            high_rows(1, 2, 0)
            with act.Fori(0, PAIRS - 1) as p:
                pair(p, 2, 2)
            pair(PAIRS - 1, 2, 1)
            pair(PAIRS, 1, 0)

        @block.tensor
        def _(pe):
            pe.wait_ge(consts_set, 5)
            pe.wait_ge(totals_done, 1)
            pe.matmul(before_p, above[:, :], totals[:, :], start=True, stop=True).then_inc(before_mm, 1)

            pe.wait_ge(over_counted, 1)
            pe.matmul(over_p, over_n[:, :], ones[:, :], start=True, stop=True).then_inc(over_mm, 1)

            pe.wait_ge(small_in, SMALL)

            def turn_xn(t, b):
                pe.wait_ge(x_normed, t + 1)
                if not isinstance(t, int) or t:
                    pe.wait_ge(xn_t_set, t)
                for c in range(KD):
                    m = pe.transpose(xn_tp[:, c, :], xn[0:T, b, c * P:(c + 1) * P], ident[0:T, 0:T])
                m.then_inc(xn_turned, 1)

            def add_kv(t, b, start=False, stop=False):
                pe.wait_ge(k_set, t + 1)
                pe.wait_ge(v_set, t + 2)
                for c in range(KD):
                    m = pe.matmul(kv_p[c], k_map[0:T, b, c * P:(c + 1) * P], v_one[0:T, b, c, :], start=start, stop=stop,
                                  skip_group_check=True)
                m.then_inc(kv_added, 1)

            def sweep1(t, b):
                if has(t + 1):
                    turn_xn(t + 1, 1 - b)
                pe.wait_ge(xn_t_set, t + 1)
                if not isinstance(t, int) or t >= 2:
                    pe.wait_ge(q_set, t - 1)
                    pe.wait_ge(v_set, t)
                if not isinstance(t, int) or t:
                    pe.wait_ge(g_copied, t)
                for c in range(KD):
                    for k in range(KD):
                        pe.matmul(q_p[b][:, c, :], wq_s[:, k, c * P:(c + 1) * P], xn_t[:, b, k, :], start=k == 0, stop=k == KD - 1)
                for o, w in ((k_p[b], wk_s), (v_p[b], wv_s), (g_p, wg_s)):
                    for k in range(KD):
                        m = pe.matmul(o[0:T, :], xn_t[:, b, k, :], w[:, k, :], start=k == 0, stop=k == KD - 1)
                m.then_inc(proj_done, 1)
                if has(t - 1):
                    add_kv(t - 1, 1 - b, start=isinstance(t, int) and t == 1)

            turn_xn(0, 0)
            over_tiles(pe, 0, 2, NT - 3, NT, sweep1)
            add_kv(NT - 1, 0, stop=True)

            def sweep2(t, b):
                if has(t + 1):
                    pe.wait_ge(q_copied, t + 2)
                    if not isinstance(t, int) or t >= 1:
                        pe.wait_ge(attn_set, t)
                    for c in range(KD):
                        m = pe.matmul(attn_p[1 - b][0:T, c, :], q_now[:, 1 - b, c, :], kv_s[:, c, :], start=True, stop=True)
                    m.then_inc(attn_mm, 1)
                if has(t):
                    pe.wait_ge(attn_set, t + 1)
                    if not isinstance(t, int) or t:
                        pe.wait_ge(attn_t_set, t)
                    for c in range(KD):
                        m = pe.transpose(xn_tp[:, c, :], attn[0:T, b, c * P:(c + 1) * P], ident[0:T, 0:T])
                    m.then_inc(attn_turned, 1)
                if has(t - 1):
                    pe.wait_ge(attn_t_set, t)
                    if not isinstance(t, int) or t >= 2:
                        pe.wait_ge(mix_set, t - 1)
                    for k in range(KD):
                        m = pe.matmul(mix_p[0:T, :], attn_t[:, 1 - b, k, :], wo_s[:, k, :], start=k == 0, stop=k == KD - 1)
                    m.then_inc(mix_mm, 1)

            pe.wait_ge(kv_ready, 1)
            sweep2(-1, 1)
            over_tiles(pe, 0, 2, NT - 1, NT + 1, sweep2)

            pe.wait_ge(stage2_done, 1)
            over_pe(pe)

            def three(o, lh, ll, rh, rl, start, stop):
                pe.matmul(o, lh, rh, start=start, stop=False)
                pe.matmul(o, lh, rl, start=False, stop=False)
                return pe.matmul(o, ll, rh, start=False, stop=stop)

            def add_blocks(p, nxt, e):
                blocks, first = part_of(nxt, e)
                for i, (b, c) in enumerate(blocks):
                    t, q = 2 * p + b, first + i
                    if q == 0 and (not isinstance(p, int) or p):
                        pe.wait_ge(x2_set, 2 * p)
                    if i == 0:
                        pe.wait_ge(onehot_set, SUM_EXPERTS * p + e + 1)
                    pe.wait_ge(rows_low, t * C + c + 1)
                    pe.matmul(agg[0:T, b, :], onehot[:, e % 2, i, :], rows_h[:, q % HIGH, :], start=c == 0, stop=False)
                    pe.matmul(agg[0:T, b, :], onehot[:, e % 2, i, :], rows[:, c, :], start=False, stop=c == C - 1).then_inc(block_added, 1)

            def turn(p, tiles):
                pe.wait_ge(normed, p + 1)
                if not isinstance(p, int) or p:
                    pe.wait_ge(y_begun, p)
                for b in range(tiles):
                    for k in range(KD):
                        m = pe.transpose(misc[:, (k * 2 + b) * T:(k * 2 + b + 1) * T],
                                         z[0:T, b, k * P:(k + 1) * P], ident[0:T, 0:T])
                m.then_inc(turned, 1)

            def hidden(p, e, n):
                x_ = p * NE + e
                if e >= 2:
                    pe.wait_ge(h_set, HC * (x_ - 1))
                for c in range(HC):
                    for k in range(KD):
                        m = three(hp[:, e % 2, c, 0:n], w1h[:, e, k, c * P:(c + 1) * P], w1l[:, e, k, c * P:(c + 1) * P],
                                  xf_h[:, k, 0:n], xf_l[:, k, 0:n], k == 0, k == KD - 1)
                    if c % 2:
                        m.then_inc(hidden_mm, 1)

            def output(p, e, tiles):
                x_ = p * NE + e
                pe.wait_ge(y_added, x_ - 1 if e else x_)
                for b in range(tiles):
                    for c in range(HC):
                        if b == 0 and c % 2 == 0:
                            pe.wait_ge(h_split, 2 * x_ + c // 2 + 1)
                        m = three(yp[0:T, e % 2, b, :], h_h[:, e % 2, c, b * T:(b + 1) * T], h_l[:, e % 2, c, b * T:(b + 1) * T],
                                  w2h[:, e, c, :], w2l[:, e, c, :], c == 0, c == HC - 1)
                m.then_inc(expert_mm, 1)

            def pair(p, tiles, nxt):
                n = W2T if tiles == 2 else T + 1
                pe.wait_ge(xf_high, p + 1)
                pe.wait_ge(xf_low, p + 1)
                for b in range(tiles):
                    for k in range(KD):
                        m = three(misc[0:T, b * NE:(b + 1) * NE], xf_h[:, k, b * T:(b + 1) * T], xf_l[:, k, b * T:(b + 1) * T],
                                  wr_h[:, k, :], wr_l[:, k, :], k == 0, k == KD - 1)
                m.then_inc(logits_mm, 1)
                for e in range(NE):
                    hidden(p, e, n)
                    if e == 1:
                        pe.wait_ge(gate_set, p + 1)
                        for b in range(tiles):
                            m = pe.transpose(misc[0:NE, b * T:(b + 1) * T], gate[0:T, b, :], ident[0:T, 0:T])
                        m.then_inc(gate_turned, 1)
                    add_blocks(p + 1, nxt, e)
                    if e == 1:
                        pe.wait_ge(gate_copied, p + 1)
                        for b in range(tiles):
                            m = pe.matmul(misc[0:T, b * D:(b + 1) * D], gate_t[:, b, :], b2_s[:, :], start=True, stop=True)
                        m.then_inc(bias_mm, 1)
                    if e:
                        output(p, e - 1, tiles)
                if nxt:
                    turn(p + 1, nxt)
                output(p, NE - 1, tiles)

            pe.wait_ge(wr_split, 2)
            pe.wait_ge(split_low, 2 * NE)
            for e in range(NE):
                add_blocks(0, 2, e)
            turn(0, 2)
            with pe.Fori(0, PAIRS - 1) as p:
                pair(p, 2, 2)
            pair(PAIRS - 1, 2, 1)
            pair(PAIRS, 1, 0)

        @block.vector
        def _(dve):
            s = Steps(dve, dve_step)
            dve.memset(src_i[96:P, LAST:J], N - 1).then_inc(pads_set, 1)
            dve.memset(dst_i[96:P, LAST:J], 0).then_inc(pads_set, 1)
            dve.memset(weight[96:P, LAST:J], 0.0).then_inc(pads_set, 1)
            dve.memset(zeros[:, :], 0.0).then_inc(zeros_set, 1)
            dve.memset(v_one[:, :, :, :], 1.0).then_inc(v_set, 1)
            dve.memset(kv_s[:, :, :], 0.0).then_inc(pads_set, 1)
            dve.wait_ge(edges_in, 16 * 6)

            dve.tensor_copy(rec[:, :, 1], weight[:, :])
            dve.tensor_copy(rec[:, :, 2].bitcast(I32), dst_i[:, :])
            s(dve.tensor_copy(src_f[:, :], src_i[:, :]))
            s(dve.tensor_scalar(tile_i[:, :], src_f[:, :], 1.0 / T, 0.5 / T, ALU.mult, ALU.add))
            s(dve.tensor_copy(tile_f[:, :], tile_i[:, :]))
            s(dve.scalar_tensor_tensor(rest[:, :], tile_f[:, :], -float(T), src_f[:, :], ALU.mult, ALU.add))
            s(dve.scalar_tensor_tensor(tile_f[:, :], rest[:, :], float(T), tile_f[:, :], ALU.is_ge, ALU.add))
            s(dve.scalar_tensor_tensor(tile_f[:, :], rest[:, :], 0.0, tile_f[:, :], ALU.is_ge, ALU.add))
            s(dve.tensor_scalar(tile_f[:, :], tile_f[:, :], -1.0, None, ALU.add))
            s(dve.scalar_tensor_tensor(rec[:, :, 0], tile_f[:, :], -float(T), src_f[:, :], ALU.mult, ALU.add))
            for t in range(NT):
                m = dve.tensor_scalar(mask[:, t, :], tile_f[:, :], float(t), None, ALU.is_equal)
            s(m)
            for t in range(NT):
                m = dve.tensor_tensor_scan(seen[:, t, :], mask[:, t, :], zeros[:, 0:J], 0.0, ALU.add, ALU.add)
            s(m)
            dve.tensor_copy(totals[:, :], seen[:, :, J - 1]).then_inc(totals_done, 1)
            dve.wait_ge(before_mm, 1)
            s(dve.tensor_scalar(before[:, :], before_p, -1.0, None, ALU.add))
            for t in range(NT):
                m = dve.scalar_tensor_tensor(mask[:, t, :], seen[:, t, :], before[:, t:t + 1], mask[:, t, :], ALU.add, ALU.mult)
            s(m)
            s(dve.tensor_reduce(rank[:, :], mask[:, :, :].rearrange("p t j -> p j t"), AX.X, ALU.add))
            s(dve.scalar_tensor_tensor(over_w[:, :], rank[:, :], float(CAP), rec[:, :, 1], ALU.is_ge, ALU.mult))
            s(dve.tensor_copy(tile_i[:, :], rank[:, :]))
            s(dve.tensor_scalar(src_i[:, :], tile_i[:, :], 7, None, ALU.logical_shift_right))
            s(dve.tensor_scalar(tile_i[:, :], tile_i[:, :], P - 1, None, ALU.bitwise_and))
            s(dve.scalar_tensor_tensor(tile_f[:, :], tile_f[:, :], float(C), src_i[:, :], ALU.mult, ALU.add))
            s(dve.scalar_tensor_tensor(tile_f[:, :], tile_i[:, :], float(NB), tile_f[:, :], ALU.mult, ALU.add))
            s(dve.tensor_scalar(rank[:, :], rank[:, :], float(CAP), float(2 * P * NB), ALU.is_ge, ALU.mult))
            dve.tensor_tensor(rec[:, :, 3].bitcast(I32), tile_f[:, :], rank[:, :], ALU.add).then_inc(records_set, 1)
            dve.memset(ones[:, :], 1.0)
            dve.tensor_reduce(over_n[:, :], rank[:, :], AX.X, ALU.max).then_inc(over_counted, 1)
            dve.wait_ge(over_mm, 1)
            dve.tensor_scalar(over_any[:, :], over_p, 1.0, None, ALU.min).then_inc(over_set, 1)
            done = s.n

            dve.wait_ge(small_in, SMALL)
            S1 = 2 + RSQRT_STEPS + 1

            def norm_x(t, b, k):
                s = Steps(dve, dve_step, done + t * S1)
                dve.wait_ge(x_loaded[b], 16 * (k + 1))
                s(dve.bn_stats(stat1[0:T, :], x_in[0:T, b, :]), dve_passed)
                s(dve.bn_aggr(mv1[0:T, :], stat1[0:T, :]))
                s(dve.tensor_scalar(rs1[0:T, 0:1], mv1[0:T, 1:2], EPS, None, ALU.add))
                rsqrt(dve, s, rs1[0:T, 0:1], rs1[0:T, 1:2], rs1[0:T, 2:3])
                assert s.n == S1
                if not isinstance(t, int) or t >= 2:
                    dve.wait_ge(xn_turned, t - 1)
                dve.tensor_scalar(xn[0:T, b, :], x_in[0:T, b, :], mv1[0:T, 0:1], rs1[0:T, 1:2], ALU.subtract, ALU.mult).then_inc(x_normed, 1)

            def sweep1(t, b, k=None):
                k = t // 2 if isinstance(t, int) else k
                if has(t + 2):
                    norm_x(t + 2, b, k + 1)
                dve.wait_ge(proj_done, t + 1)
                if not isinstance(t, int) or t:
                    dve.wait_ge(k_set, t)
                dve.tensor_tensor(k_z[0:T, :], k_p[b][0:T, :], bk_s[0:T, :], ALU.add).then_inc(k_zed, 1)
                if not isinstance(t, int) or t >= 2:
                    dve.wait_ge(kv_added, t - 1)
                dve.tensor_tensor(v_one[0:T, b, :, 0:P], v_p[b][0:T, :].rearrange("p (c n) -> p c n", c=KD),
                                  bv_s[0:T, :].rearrange("p (c n) -> p c n", c=KD), ALU.add).then_inc(v_set, 1)
                dve.wait_ge(q_exped, KD * (t + 1))
                for c in range(KD):
                    m = dve.tensor_scalar(q_pos[:, c, :], q_p[b][:, c, :], bq_s[:, c:c + 1], 0.0, ALU.add, ALU.max)
                m.then_inc(q_pos_set, 1)
                dve.wait_ge(q_pos_set, t + 1)
                dve.scalar_tensor_tensor(q_t[:, :, bass.ds(t * T, T)], q_exp[:, :, :], 1.0, q_pos[:, :, :], ALU.min, ALU.add).then_inc(q_set, 1)
                dve.wait_ge(k_exped, t + 1)
                dve.tensor_scalar(k_z[0:T, :], k_z[0:T, :], 0.0, None, ALU.max).then_inc(k_pos_set, 1)
                dve.wait_ge(k_pos_set, t + 1)
                dve.scalar_tensor_tensor(k_map[0:T, b, :], k_exp[0:T, :], 1.0, k_z[0:T, :], ALU.min, ALU.add).then_inc(k_set, 1)

            norm_x(0, 0, 0)
            norm_x(1, 1, 0)
            for t in range(2):
                sweep1(t, t)
            with dve.Fori(1, (NT - 3) // 2) as i:
                sweep1(2 * i, 0, i)
                sweep1(2 * i + 1, 1, i)
            for t in range(NT - 3, NT):
                sweep1(t, t % 2)
            done = done + NT * S1

            dve.wait_ge(kv_added, NT)
            for c in range(KD):
                for g in range(P // HD):
                    r = slice(g * HD, (g + 1) * HD)
                    dve.tensor_copy(kv_s[r, c, r], kv_p[c][r, r])
                    m = dve.tensor_copy(kv_s[r, c, P + g:P + g + 1], kv_p[c][r, P:P + 1])
            m.then_inc(kv_ready, 1)

            S2 = 1

            def sweep2(t, b, k=None, split=None):
                k = t // 2 if isinstance(t, int) else k
                if has(t + 1):
                    s = Steps(dve, dve_step, done + (t + 1) * S2)
                    dve.wait_ge(attn_mm, t + 2)
                    if not isinstance(t, int) or t >= 0:
                        dve.wait_ge(attn_set, t + 1)
                    now = attn_p[1 - b]
                    s(dve.tensor_scalar(norm[0:T, :].rearrange("p (c g) -> p c g", c=KD), now[0:T, :, P:NK], 1e-6, None, ALU.add))
                    assert s.n == S2
                    dve.reciprocal(norm[0:T, :], norm[0:T, :]).then_inc(norm_set, 1)
                    dve.wait_ge(norm_set, t + 2)
                    if not isinstance(t, int) or t >= 1:
                        dve.wait_ge(attn_turned, t)
                    for c in range(KD):
                        g = P // HD
                        m = dve.tensor_tensor(attn[0:T, 1 - b, c * P:(c + 1) * P].rearrange("p (g d) -> p g d", g=g),
                                              now[0:T, c, 0:P].rearrange("p (g d) -> p g d", g=g),
                                              norm[0:T, c * g:(c + 1) * g].unsqueeze(2).to_broadcast([T, g, HD]), ALU.mult)
                    m.then_inc(attn_set, 1)
                if has(t - 1):
                    dve.wait_ge(x_loaded[b], 16 * ((NT + 1) // 2 + k if b == 0 else NT // 2 + k + 1))
                    dve.tensor_tensor(x_in[0:T, b, :], x_in[0:T, b, :], bo_s[0:T, :], ALU.add).then_inc(x_biased, 1)
                    dve.wait_ge(x_biased, t)
                    dve.wait_ge(mix_mm, t)
                    if not isinstance(t, int) or t >= 3:
                        dve.wait_ge(mix_stored[b], 16 * (k - 1 + b))
                    dve.tensor_tensor(mix_out[0:T, b, :], mix_p[0:T, :], x_in[0:T, b, :], ALU.add).then_inc(mix_set, 1)
                if split is not None:
                    wh, wl = ((w1h, w1l), (w2h, w2l))[b]
                    dve.wait_ge(split_high, 2 * split + b + 1)
                    dve.tensor_tensor(wl[:, bass.ds(split, 1), :, :].rearrange("p e k n -> p (e k n)"), stage[:, b, :],
                                      wh[:, bass.ds(split, 1), :, :].rearrange("p e k n -> p (e k n)").bitcast(F32),
                                      ALU.subtract).then_inc(split_low, 1)

            sweep2(-1, 1)
            for t in range(2):
                sweep2(t, t)
            with dve.Fori(1, NE) as i:
                sweep2(2 * i, 0, i, i - 1)
                sweep2(2 * i + 1, 1, i, i - 1)
            for t in range(2 * NE, 2 * NE + 2):
                sweep2(t, t % 2, split=NE - 1)
            for t in range(2 * NE + 2, NT + 1):
                sweep2(t, t % 2)
            done = done + NT * S2
            dve.wait_ge(wr_split, 1)
            dve.tensor_tensor(wr_l[:, :, :], wr_s[:, :, :], wr_h[:, :, :].bitcast(F32), ALU.subtract).then_inc(wr_split, 1)

            dve.wait_ge(mix_stored[0], 16 * (NT // 2))
            dve.wait_ge(mix_stored[1], 16 * (NT // 2 + 1))
            dve.wait_ge(chunk_out[0], 16 * C * (CH // 2 + 1))
            dve.wait_ge(chunk_out[1], 16 * C * (CH // 2))
            dve.memset(mv[:, :, :], 0.0).then_inc(stage2_done, 1)

            over_dve(dve)

            def low_rows(p, nxt, e):
                blocks, first = part_of(nxt, e)
                for b in sorted({b for b, c in blocks}):
                    cs = [c for b_, c in blocks if b_ == b]
                    i, n = blocks.index((b, cs[0])), len(cs)
                    if cs[0] == 0:
                        dve.wait_ge(slots_in[b], 16 * (p + 1))
                    if i == 0 and (e >= 2 or not isinstance(p, int) or p):
                        dve.wait_ge(block_added, 2 * p * C + max(e - 1, 0) * PART)
                    m = dve.tensor_tensor(onehot[:, e % 2, i:i + n, :], iota_row[:, :].unsqueeze(1).to_broadcast([P, n, T]),
                                          slot_rec[:, b, cs[0]:cs[-1] + 1, 0:1].to_broadcast([P, n, T]), ALU.is_equal)
                if blocks:
                    m.then_inc(onehot_set, 1)
                for b, c in blocks:
                    dve.wait_ge(rows_high, (2 * p + b) * C + c + 1)
                    dve.scalar_tensor_tensor(rows[:, c, :], rows[:, c, :].bitcast(F32), slot_rec[:, b, c, 1:2],
                                             rows_h[:, (first + blocks.index((b, c))) % HIGH, :].bitcast(F32),
                                             ALU.mult, ALU.subtract).then_inc(rows_low, 1)

            def norms(p, tiles, s, part):
                def moments(now):
                    for b in range(tiles):
                        m = dve.bn_stats(stat[0:T, b, :], now[0:T, b, :])
                    s(m, dve_passed)
                    for b in range(tiles):
                        m = dve.bn_aggr(mv[0:T, b, :], stat[0:T, b, :])
                    s(m)
                    s(dve.tensor_scalar(rs[0:T, 0, :], mv[0:T, :, 1], EPS, None, ALU.add))
                    rsqrt(dve, s, rs[0:T, 0, :], rs[0:T, 1, :], rs[0:T, 2, :])

                if part == 0:
                    dve.wait_ge(block_added, (2 * p + tiles) * C)
                    for b in range(tiles):
                        dve.wait_ge(rest_in[b], 32 * (p + 1))
                        m = dve.tensor_tensor(z[0:T, b, :], agg[0:T, b, :], extra_in[0:T, b, :], ALU.add)
                    s(m)
                    for b in range(tiles):
                        dve.scalar_tensor_tensor(x2[0:T, b, :], z[0:T, b, :], 0.0, mixed_in[0:T, b, :], ALU.max, ALU.add).then_inc(x2_set, 1)
                    dve.wait_ge(x2_set, 2 * p + tiles)
                    moments(x2)
                if part == 1:
                    for b in range(tiles):
                        m = dve.tensor_scalar(z[0:T, b, :], x2[0:T, b, :], mv[0:T, b, 0:1], rs[0:T, 1, b:b + 1],
                                              ALU.subtract, ALU.mult)
                    s(m)
                    moments(z)
                if part == 2:
                    for b in range(tiles):
                        m = dve.scalar_tensor_tensor(z[0:T, b, :], z[0:T, b, :], mv[0:T, b, 0:1], gamma_s[0:T, :], ALU.subtract, ALU.mult)
                    s(m)
                    for b in range(tiles):
                        m = dve.scalar_tensor_tensor(z[0:T, b, :], z[0:T, b, :], rs[0:T, 1, b:b + 1], beta_s[0:T, :], ALU.mult, ALU.add)
                    m.then_inc(normed, 1)

            def norm_steps(tiles):
                return 1 + 2 * (3 + RSQRT_STEPS) + 2

            def low_halves(p):
                dve.wait_ge(xf_high, p + 1)
                dve.tensor_tensor(xf_l[:, :, :].rearrange("p k n -> p (k n)"), misc[:, 0:KD * W2T],
                                  xf_h[:, :, :].rearrange("p k n -> p (k n)").bitcast(F32), ALU.subtract).then_inc(xf_low, 1)

            ROUTE = 10

            def route(p, tiles, s, part):
                if part == 0:
                    dve.wait_ge(logits_mm, p + 1)
                    s(dve.tensor_tensor(logit[0:T, 0:tiles, :], misc[0:T, 0:tiles * NE].rearrange("p (b e) -> p b e", b=tiles),
                                        br_s[0:T, :].unsqueeze(1).to_broadcast([T, tiles, NE]), ALU.add), dve_passed)
                    for b in range(tiles):
                        m = dve.max(top[0:T, b, :], logit[0:T, b, :])
                    s(m)
                    dve.tensor_tensor(share[0:T, 0:tiles, 0:1], top[0:T, 0:tiles, 0:1], top[0:T, 0:tiles, 1:2],
                                      ALU.subtract).then_inc(diff_set, 1)
                    for b in range(tiles):
                        m = dve.max_index(top_at[0:T, b, :], top[0:T, b, :], logit[0:T, b, :])
                    s(m)
                    s(dve.tensor_copy(top_f[0:T, 0:tiles, 0:2], top_at[0:T, 0:tiles, 0:2]))
                else:
                    dve.wait_ge(tanh_set, p + 1)
                    dve.tensor_scalar(share[0:T, 0:tiles, 2:3], share[0:T, 0:tiles, 1:2], 0.5, 0.5, ALU.mult, ALU.add)
                    s(dve.tensor_scalar(share[0:T, 0:tiles, 3:4], share[0:T, 0:tiles, 1:2], -0.5, 0.5, ALU.mult, ALU.add))
                    for b in range(tiles):
                        m = dve.tensor_scalar(gate[0:T, b, :], iota_row[0:T, 0:NE], top_f[0:T, b, 0:1], share[0:T, b, 2:3],
                                              ALU.is_equal, ALU.mult)
                    s(m)
                    for b in range(tiles):
                        m = dve.tensor_scalar(logit[0:T, b, :], iota_row[0:T, 0:NE], top_f[0:T, b, 1:2], share[0:T, b, 3:4],
                                              ALU.is_equal, ALU.mult)
                    s(m)
                    dve.tensor_tensor(gate[0:T, 0:tiles, :], gate[0:T, 0:tiles, :], logit[0:T, 0:tiles, :], ALU.add).then_inc(gate_set, 1)
                    dve.wait_ge(gate_set, p + 1)

            ROUTE_STEPS = 7

            def split(p, e, n):
                x_ = p * NE + e
                if e >= 2:
                    dve.wait_ge(expert_mm, x_ - 1)
                for g in range(2):
                    r = slice(2 * g, 2 * g + 2)
                    dve.wait_ge(h_high, 2 * x_ + g + 1)
                    dve.tensor_tensor(h_l[:, e % 2, r, 0:n], h[:, r, 0:n], h_h[:, e % 2, r, 0:n].bitcast(F32), ALU.subtract).then_inc(h_split, 1)

            def begin_y(p, tiles):
                dve.wait_ge(bias_mm, p + 1)
                if not isinstance(p, int) or p:
                    dve.wait_ge(y_stored, 16 * 2 * p)
                dve.tensor_tensor(y[0:T, 0:tiles, :], misc[0:T, 0:tiles * D].rearrange("p (b n) -> p b n", b=tiles),
                                  x2[0:T, 0:tiles, :], ALU.add).then_inc(y_begun, 1)
                dve.wait_ge(y_begun, p + 1)

            def add_y(p, e, tiles):
                x_ = p * NE + e
                dve.wait_ge(expert_mm, x_ + 1)
                for b in range(tiles):
                    m = dve.scalar_tensor_tensor(y[0:T, b, :], yp[0:T, e % 2, b, :], gate[0:T, b, e:e + 1], y[0:T, b, :],
                                                 ALU.mult, ALU.add)
                m.then_inc(y_added, 1)
                dve.wait_ge(y_added, x_ + 1)

            def pair(p, tiles, nxt, s):
                n = W2T if tiles == 2 else T + 1
                for e in range(NE):
                    if e == 0:
                        route(p, tiles, s, 0)
                    split(p, e, n)
                    if e == 0:
                        route(p, tiles, s, 1)
                    low_rows(p + 1, nxt, e + 1)
                    if e == 1:
                        begin_y(p, tiles)
                    if e:
                        add_y(p, e - 1, tiles)
                    if nxt and 0 <= e - NORM_FROM < 3:
                        norms(p + 1, nxt, s, e - NORM_FROM)
                if nxt:
                    low_halves(p + 1)
                if nxt == 2:
                    low_rows(p + 2, 1, 0)
                add_y(p, NE - 1, tiles)

            s = Steps(dve, dve_step, done)
            for e in range(NE):
                low_rows(0, 2, e)
            for part in range(3):
                norms(0, 2, s, part)
            low_halves(0)
            low_rows(1, 2, 0)
            done = done + s.n
            PER = ROUTE_STEPS + norm_steps(2)
            with dve.Fori(0, PAIRS - 1) as p:
                s = Steps(dve, dve_step, done + p * PER)
                pair(p, 2, 2, s)
                assert s.n == PER, s.n
            done = done + (PAIRS - 1) * PER
            s = Steps(dve, dve_step, done)
            pair(PAIRS - 1, 2, 1, s)
            pair(PAIRS, 1, 0, s)


_INS = ["x", "src", "dst", "edge_weight", "L0_gnn_weight", "L0_mix_wq", "L0_mix_bq", "L0_mix_wk", "L0_mix_bk",
        "L0_mix_wv", "L0_mix_bv", "L0_mix_wo", "L0_mix_bo", "L0_ffn_gamma", "L0_ffn_beta", "L0_ffn_Wr",
        "L0_ffn_br", "L0_ffn_W1", "L0_ffn_b1", "L0_ffn_W2", "L0_ffn_b2"]


def kernel(**inputs):
    import numpy as _np
    import concourse.bacc as _bacc
    from concourse import mybir as _mybir
    from concourse.bass_utils import run_bass_kernel_spmd as _run

    nc = _bacc.Bacc("TRN2", target_bir_lowering=False, num_devices=1)
    arrays, args = {}, []
    for name in _INS:
        a = _np.ascontiguousarray(inputs[name])
        arrays[f"in_{name}"] = a
        args.append(nc.dram_tensor(f"in_{name}", a.shape, _mybir.dt.from_np(a.dtype), kind="ExternalInput").ap())
    args.append(nc.dram_tensor("out_0", (N, D), F32, kind="ExternalOutput").ap())
    build(nc, *args)
    r = _run(nc, [arrays], core_ids=[0])
    return r.results[0]["out_0"]
```

```python
from contextlib import ExitStack

import concourse.bass as bass
from concourse import mybir

F32, F32R, I32, U32 = mybir.dt.float32, mybir.dt.float32r, mybir.dt.int32, mybir.dt.uint32
ALU = mybir.AluOpType
ACT = mybir.ActivationFunctionType
AX = mybir.AxisListType

P = 128
N, D = 3125, 256
T = 125
NT = N // T
E = 50000
J = -(-E // P)
LAST = E - (P - 1) * J
C = 17
CAP = C * P
NB = NT * C
CH = 19
LO = CH * C
JP = J - LO
DEPTH = 6
WAYS = 4
NQ = -(-NB // WAYS)
HEADS, HD = 8, 32
NE, HID = 8, 512
HC = HID // P
KD = D // P
W2T = 2 * T
PAIRS = NT // 2
SUM_EXPERTS = 6
PART = -(-2 * C // SUM_EXPERTS)
NORM_FROM = 4
HIGH = PART
EPS = 1e-5
RSQRT_BITS = 0x5F3759DF
assert NT % 2 == 1 and NT * T == N


def apart(eng, passed):
    eng.sem_inc(passed, 1)


def has(t):
    return not isinstance(t, int) or 0 <= t < NT


def over_tiles(eng, first, lo, hi, last, step):
    for t in range(first, lo):
        step(t, t % 2)
    with eng.Fori(lo // 2, hi // 2) as i:
        step(2 * i, 0)
        step(2 * i + 1, 1)
    for t in range(hi, last):
        step(t, t % 2)


def over_columns(eng, step):
    for j in range(DEPTH):
        step(j, j)
    with eng.Fori(1, (JP - 1) // DEPTH) as i:
        for u in range(DEPTH):
            step(DEPTH * i + u, u)
    for j in range((JP - 1) // DEPTH * DEPTH, JP):
        step(j, j % DEPTH)


class Steps:

    def __init__(self, eng, sem, before=0):
        self.eng, self.sem, self.before, self.n = eng, sem, before, 0

    def __call__(self, ins, passed=None):
        self.n += 1
        ins.then_inc(self.sem, 1)
        self.eng.wait_ge(self.sem, self.before + self.n)
        if passed is not None:
            apart(self.eng, passed)


def rsqrt(eng, s, v, y, a):
    s(eng.tensor_scalar(y.bitcast(I32), v.bitcast(I32), 1, None, ALU.logical_shift_right))
    s(eng.tensor_scalar(y.bitcast(I32), y.bitcast(I32), -1.0, float(RSQRT_BITS), ALU.mult, ALU.add))
    for _ in range(3):
        s(eng.scalar_tensor_tensor(a, y, -0.5, y, ALU.mult, ALU.mult))
        s(eng.tensor_tensor(a, a, v, ALU.mult))
        s(eng.scalar_tensor_tensor(y, a, 1.5, y, ALU.add, ALU.mult))


RSQRT_STEPS = 11


def build(nc, x, src, dst, edge_weight, w_gnn, wq, bq, wk, bk, wv, bv, wo, bo, gamma, beta, Wr, br,
          W1, b1, W2, b2, out):
    ctx = ExitStack()
    with ctx:
        def sb(name, shape, dt=F32, where=ctx):
            return where.enter_context(nc.sbuf_tensor(name, shape, dt))

        def sem(name):
            return ctx.enter_context(nc.semaphore(name))

        slots = nc.dram_tensor("slots", (P * NB, 4), F32, kind="Internal").ap()
        placed = nc.dram_tensor("placed", (P, NB, 4), F32, kind="Internal").ap()
        slots_by_lane = slots.rearrange("(p b) r -> p b r", p=P)
        table = nc.dram_tensor("table", (N, D), F32, kind="Internal").ap()
        mixed = nc.dram_tensor("mixed", (N, D), F32, kind="Internal").ap()
        extra = nc.dram_tensor("extra", (N, D), F32, kind="Internal").ap()

        iota_row = sb("iota_row", [P, T])
        ident = sb("ident", [P, P])
        over_n = sb("over_n", [P, 1])
        over_any = sb("over_any", [1, 1], I32)
        ones = sb("ones", [P, 1])

        with ExitStack() as early:
            src_i = sb("src_i", [P, J], I32, early)
            dst_i = sb("dst_i", [P, J], I32, early)
            weight = sb("weight", [P, J], F32, early)
            tile_i = sb("tile_i", [P, J], I32, early)
            tile_f = sb("tile_f", [P, J], F32, early)
            rest = sb("rest", [P, J], F32, early)
            zeros = sb("zeros", [P, 1700], F32, early)
            mask = sb("mask", [P, NT, J], F32, early)
            seen = sb("seen", [P, NT, J], F32, early)
            rank = sb("rank", [P, J], F32, early)
            above = sb("above", [P, P], F32, early)
            totals = sb("totals", [P, NT], F32, early)
            before = sb("before", [P, NT], F32, early)
        w1h = sb("w1h", [P, NE, KD, HID], F32R)
        w1l = sb("w1l", [P, NE, KD, HID], F32R)
        w2h = sb("w2h", [P, NE, HC, D], F32R)
        w2l = sb("w2l", [P, NE, HC, D], F32R)

        gamma_s, beta_s = sb("gamma_s", [P, D]), sb("beta_s", [P, D])
        br_s = sb("br_s", [P, NE])
        b1_s = sb("b1_s", [P, NE, HC])
        b2_s = sb("b2_s", [NE, D])
        wr_s = sb("wr_s", [P, KD, NE])
        wr_h = sb("wr_h", [P, KD, NE], F32R)
        wr_l = sb("wr_l", [P, KD, NE], F32R)

        edges = ExitStack()
        rec = sb("rec", [P, J, 4], F32, edges)
        over_w = sb("over_w", [P, J], F32, edges)
        slot_a = sb("slot_a", [P, JP], F32, edges)
        slot_b = sb("slot_b", [P, JP], F32, edges)
        row_now = sb("row_now", [P, 1], F32, edges)
        col_now = sb("col_now", [P, 1], I32, edges)
        src_f = sb("src_f", [P, J], F32, edges)
        with ExitStack() as mid:
            q_t = sb("q_t", [P, KD, N], F32, mid)
            wq_s, wk_s, wv_s, wo_s, wg_s = (sb(n, [P, KD, D], F32, mid)
                                            for n in ("wq_s", "wk_s", "wv_s", "wo_s", "wg_s"))
            bk_s, bv_s, bo_s = (sb(n, [P, D], F32, mid) for n in ("bk_s", "bv_s", "bo_s"))
            bq_s = sb("bq_s", [P, KD], F32, mid)
            x_in = sb("x_in", [P, 2, D], F32, mid)
            xn = sb("xn", [P, 2, D], F32, mid)
            xn_t = sb("xn_t", [P, 2, KD, T], F32, mid)
            stat1 = sb("stat1", [P, 2, 6], F32, mid)
            mv1 = sb("mv1", [P, 2, 2], F32, mid)
            rs1 = sb("rs1", [P, 3, 2], F32, mid)
            q_exp = sb("q_exp", [P, KD, T], F32, mid)
            q_pos = sb("q_pos", [P, KD, T], F32, mid)
            k_z = sb("k_z", [P, D], F32, mid)
            k_exp = sb("k_exp", [P, D], F32, mid)
            k_map = sb("k_map", [P, 2, D], F32, mid)
            v_one = sb("v_one", [P, 2, KD, P + 1], F32, mid)
            g_out = sb("g_out", [P, 2, D], F32, mid)
            kv_s = sb("kv_s", [P, KD, P + HEADS // KD], F32, mid)
            q_now = xn_t
            norm = sb("norm", [P, HEADS], F32, mid)
            attn = xn
            attn_t = sb("attn_t", [P, 2, KD, T], F32, mid)
            k_pos = attn_t[:, :, :, :].rearrange("p a k n -> p (a k n)")[:, 0:D]
            mix_out = k_map
            rec_buf = sb("rec_buf", [P, 2, C, 4], F32, mid)
            stage = sb("stage", [P, 2, NE // 4 * D * 2], F32, mid)
        with ExitStack() as late:
            iota_a = sb("iota_a", [P, WAYS * P], F32, late)
            hot_a = sb("hot_a", [P, DEPTH, WAYS * P], F32R, late)
            hot_b = sb("hot_b", [P, DEPTH, NQ], F32, late)
            fields = sb("fields", [P, DEPTH, 4, NQ], F32R, late)
            weight_h = sb("weight_h", [P, JP], F32R, late)
            weight_l = sb("weight_l", [P, JP], F32, late)
            sums = sb("sums", [P, NQ, WAYS, 4], F32, late)
        with ExitStack() as between:
            over_acc = sb("over_acc", [P, NT, D], F32, between)
            over_rows = sb("over_rows", [P, D], F32, between)
            hot_now = sb("hot_now", [P, T], F32, between)
        edges.close()
        rows = sb("rows", [P, C, D], F32R)
        rows_h = sb("rows_h", [P, HIGH, D], F32R)
        onehot = sb("onehot", [P, 2, PART, T], F32R)
        slot_rec = sb("slot_rec", [P, 2, C, 4])
        slot_more = sb("slot_more", [P, 2, C, 4])
        slot_col = sb("slot_col", [P, 2, C], I32)
        mixed_in = sb("mixed_in", [P, 2, D])
        extra_in = sb("extra_in", [P, 2, D])
        x2 = sb("x2", [P, 2, D])
        z = sb("z", [P, 2, D])
        stat = sb("stat", [P, 2, 6])
        mv = sb("mv", [P, 2, 2])
        rs = sb("rs", [P, 3, 2])
        xf_h = sb("xf_h", [P, KD, W2T], F32R)
        xf_l = sb("xf_l", [P, KD, W2T], F32R)
        h = sb("h", [P, HC, W2T])
        h_h = sb("h_h", [P, 2, HC, W2T], F32R)
        h_l = sb("h_l", [P, 2, HC, W2T], F32R)
        logit = sb("logit", [P, 2, NE])
        top = sb("top", [P, 2, NE])
        top_at = sb("top_at", [P, 2, NE], U32)
        top_f = sb("top_f", [P, 2, NE])
        share = sb("share", [P, 2, 4])
        gate = sb("gate", [P, 2, NE])
        gate_t = sb("gate_t", [NE, 2, T])
        y = sb("y", [P, 2, D])
        hp = ctx.enter_context(nc.psum_tensor("hp", [P, 2, HC, 256], F32))
        yp = ctx.enter_context(nc.psum_tensor("yp", [P, 2, 2, D], F32))
        agg = ctx.enter_context(nc.psum_tensor("agg", [P, 2, D], F32))
        misc = ctx.enter_context(nc.psum_tensor("misc", [P, 512], F32))
        banks = hp[:, :, :, :].rearrange("p a (b c) n -> p (a b) (c n)", b=2)
        q_p = [b[:, 0:W2T].rearrange("p (c n) -> p c n", c=KD) for b in (banks[:, 0, :], misc[:, :])]
        kv_now = [banks[:, 1, :], agg[:, :, :].rearrange("p a n -> p (a n)")]
        k_p, v_p = [b[:, 0:D] for b in kv_now], [b[:, D:2 * D] for b in kv_now]
        g_p = banks[:, 2, 0:D]
        mix_p = banks[:, 2, 0:D]
        xn_tp = banks[:, 3, 0:W2T].rearrange("p (c n) -> p c n", c=KD)
        over_p = misc[0:1, 0:1]
        before_p = banks[:, 3, 0:NT]
        NK = P + HEADS // KD
        attn_p = [banks[:, b, 0:KD * NK].rearrange("p (c n) -> p c n", c=KD) for b in range(2)]
        kv_p = [yp[:, c, :, :].rearrange("p a n -> p (a n)")[:, 0:P + 1] for c in range(KD)]

        place_p = [yp[:, 0, :, :].rearrange("p a n -> p (a n)"), yp[:, 1, :, :].rearrange("p a n -> p (a n)"),
                   agg[:, :, :].rearrange("p a n -> p (a n)"), misc[:, :]]

        (pads_set, edges_in, zeros_set, zeros_out, consts_set, totals_done, before_mm, records_set,
         dve_step) = map(sem, ("pads_set", "edges_in", "zeros_set", "zeros_out", "consts_set",
                               "totals_done", "before_mm", "records_set", "dve_step"))
        chunk_in = [sem(f"chunk_in{i}") for i in range(2)]
        chunk_out = [sem(f"chunk_out{i}") for i in range(2)]
        (small_in, x_loaded0, x_loaded1, x_normed, xn_turned, xn_t_set, proj_done, q_exped, k_zed,
         k_exped, k_set, v_set, q_set, g_copied, kv_added) = map(sem, (
             "small_in", "x_loaded0", "x_loaded1", "x_normed", "xn_turned", "xn_t_set", "proj_done",
             "q_exped", "k_zed", "k_exped", "k_set", "v_set", "q_set", "g_copied",
             "kv_added"))
        g_stored = [sem(f"g_stored{i}") for i in range(2)]
        x_loaded = [x_loaded0, x_loaded1]
        kv_ready, split_in0, split_in1, split_high, split_low = map(sem, (
            "kv_ready", "split_in0", "split_in1", "split_high", "split_low"))
        split_in = [split_in0, split_in1]
        q_copied, attn_mm, attn_set, attn_turned, attn_t_set, mix_mm, mix_set = map(
            sem, ("q_copied", "attn_mm", "attn_set", "attn_turned", "attn_t_set", "mix_mm",
                  "mix_set"))
        mix_stored = [sem(f"mix_stored{i}") for i in range(2)]
        slots_in = [sem(f"slots_in{i}") for i in range(2)]
        rest_in = [sem(f"rest_in{i}") for i in range(2)]
        row_in = [sem(f"row_in{c}") for c in range(C)]
        onehot_set, block_added, x2_set, normed, turned, xf_high, xf_low = map(sem, (
            "onehot_set", "block_added", "x2_set", "normed", "turned", "xf_high",
            "xf_low"))
        (logits_mm, diff_set, tanh_set, gate_set, gate_turned, gate_copied, bias_mm, y_begun,
         hidden_mm, h_set, h_high, h_split, expert_mm, y_added, y_stored) = map(sem, (
             "logits_mm", "diff_set", "tanh_set", "gate_set", "gate_turned", "gate_copied",
             "bias_mm", "y_begun", "hidden_mm", "h_set", "h_high", "h_split", "expert_mm",
             "y_added", "y_stored"))
        stage2_done = sem("stage2_done")
        over_counted, over_mm, over_set = sem("over_counted"), sem("over_mm"), sem("over_set")
        (over_col, over_row, over_hot, over_sum, over_added, over_row_set, over_stored, over_step) = map(sem, (
            "over_col", "over_row", "over_hot", "over_sum", "over_added", "over_row_set", "over_stored",
            "over_step"))
        norm_set, x_biased = sem("norm_set"), sem("x_biased")
        pool_passed, dve_passed, pe_passed = sem("pool_passed"), sem("dve_passed"), sem("pe_passed")
        wr_split = sem("wr_split")
        (halved, hot_a_set, hot_b_set, fields_set, col_placed, sums_set, sums_out, slots_set) = map(sem, (
            "halved", "hot_a_set", "hot_b_set", "fields_set", "col_placed", "sums_set", "sums_out", "slots_set"))
        slots_summed = sem("slots_summed")
        rows_high, rows_low = sem("rows_high"), sem("rows_low")

        def part_of(nxt, e):
            return [(b, c) for b in range(nxt) for c in range(C)][e * PART:(e + 1) * PART], e * PART

        block = ctx.enter_context(nc.Block())
        SMALL = 16 * 15

        def when_over(eng):
            eng.wait_ge(over_set, 1)
            return eng.If(eng.value_load(over_any[0:1, 0:1], min_val=0, max_val=1) > 0)

        def over_pool(pool):
            with when_over(pool):
                with pool.Fori(0, J) as j:
                    pool.wait_ge(over_col, j + 1)
                    apart(pool, pool_passed)
                    pool.indirect_dma_start(over_rows[:, :], None, table,
                                            bass.IndirectOffsetOnAxis(ap=col_now[:, 0:1], axis=0)).then_inc(over_row, 16)

        def over_pe(pe):
            with when_over(pe):
                with pe.Fori(0, J) as j:
                    pe.wait_ge(over_row, 16 * (j + 1))
                    apart(pe, pe_passed)
                    with pe.Fori(0, NT) as t:
                        pe.wait_ge(over_hot, j * NT + t + 1)
                        pe.matmul(agg[0:T, 0, :], hot_now[:, :], over_rows[:, :], start=True, stop=True).then_inc(over_sum, 1)

        def over_sp(sp):
            with when_over(sp):
                sp.wait_ge(over_added, NT * J + 1)
                sp.dma_start(extra.rearrange("(t p) n -> p t n", p=T), over_acc[0:T, :, :]).then_inc(over_stored, 16)
                sp.wait_ge(over_stored, 16)

        def over_dve(dve):
            with when_over(dve):
                dve.memset(over_acc[:, :, :], 0.0).then_inc(over_added, 1)
                dve.wait_ge(over_added, 1)
                with dve.Fori(0, J) as j:
                    dve.tensor_copy(col_now[:, :], rec[:, bass.ds(j, 1), 2]).then_inc(over_col, 1)
                    dve.tensor_copy(row_now[:, :], src_f[:, bass.ds(j, 1)]).then_inc(over_row_set, 1)
                    dve.wait_ge(over_row_set, j + 1)
                    apart(dve, dve_passed)
                    with dve.Fori(0, NT) as t:
                        q = j * NT + t
                        dve.tensor_scalar(hot_now[:, :], iota_row[:, :], row_now[:, 0:1], over_w[:, bass.ds(j, 1)],
                                          ALU.is_equal, ALU.mult).then_inc(over_hot, 1)
                        dve.wait_ge(over_hot, q + 1)
                        dve.tensor_scalar(row_now[:, :], row_now[:, :], -float(T), None, ALU.add).then_inc(over_step, 1)
                        dve.wait_ge(over_step, q + 1)
                        dve.wait_ge(over_sum, q + 1)
                        dve.tensor_tensor(over_acc[0:T, bass.ds(t, 1), :], over_acc[0:T, bass.ds(t, 1), :],
                                          agg[0:T, 0:1, :], ALU.add).then_inc(over_added, 1)
                        dve.wait_ge(over_added, q + 2)
                        apart(dve, dve_passed)
                dve.wait_ge(over_stored, 16)

        def by_chunk(w):
            return w.rearrange("(k p) n -> p k n", p=P)

        def to_rows(b):
            return b.rearrange("(a n) -> a n", a=1).to_broadcast([P, b.shape[0]])

        @block.sync
        def _(sp):
            sp.wait_ge(pads_set, 3)
            for t, v in ((src_i, src), (dst_i, dst), (weight, edge_weight)):
                sp.dma_start(t[0:P - 1, :], v[0:(P - 1) * J].rearrange("(p j) -> p j", p=P - 1)).then_inc(edges_in, 16)
                sp.dma_start(t[P - 1:P, 0:LAST], v[(P - 1) * J:E].rearrange("(p j) -> p j", p=1)).then_inc(edges_in, 16)
            sp.wait_ge(zeros_set, 1)
            sp.dma_start(slots_by_lane.rearrange("p b r -> p (b r)"), zeros[:, 0:NB * 4]).then_inc(zeros_out, 16)
            for i in range(4):
                w = N * D // T // 4
                sp.dma_start(extra.rearrange("(p a) n -> p (a n)", p=T)[:, i * w:(i + 1) * w],
                             zeros[0:T, 0:w]).then_inc(zeros_out, 16)

            def chunk(c, b, k):
                sp.dma_start(rec_buf[:, b, :, :].rearrange("p c r -> p (c r)"),
                             rec[:, bass.ds(c * C, C), :].rearrange("p c r -> p (c r)"))\
                    .then_inc(chunk_in[b], 16)

            sp.wait_ge(records_set, 1)
            chunk(0, 0, 0)
            chunk(1, 1, 0)
            sp.wait_ge(records_set, 2)
            with sp.Fori(1, CH // 2) as i:
                for b in range(2):
                    sp.wait_ge(chunk_out[b], 16 * C * i)
                    chunk(2 * i + b, b, i)
            if CH % 2:
                sp.wait_ge(chunk_out[0], 16 * C * (CH // 2))
                chunk(CH - 1, 0, CH // 2)

            sp.wait_ge(sums_set, 1)
            sp.dma_start(placed.rearrange("p b r -> p (b r)"),
                         sums[:, :, :, :].rearrange("p q w r -> p (q w r)")[:, 0:NB * 4]).then_inc(sums_out, 16)

            sp.wait_ge(chunk_out[0], 16 * C * (CH - CH // 2))
            sp.wait_ge(chunk_out[1], 16 * C * (CH // 2))
            sp.wait_ge(zeros_out, 16 * 5)
            sp.wait_ge(mix_stored[0], 16 * (NT // 2))
            sp.wait_ge(mix_stored[1], 16 * (NT // 2 + 1))
            for b in range(2):
                sp.wait_ge(g_stored[b], 16 * ((NT + 1 - b) // 2))

            sp.wait_ge(stage2_done, 1)
            over_sp(sp)

            def load(t, b, k, first=False):
                if not first:
                    sp.wait_ge(block_added, (t - 1) * C)
                sp.dma_start(slot_rec[:, b, :, :].rearrange("p c r -> p (c r)"),
                             slots_by_lane[:, bass.ds(t * C, C), :].rearrange("p c r -> p (c r)"))\
                    .then_inc(slots_in[b], 16)
                sp.dma_start(slot_more[:, b, :, :].rearrange("p c r -> p (c r)"),
                             placed[:, bass.ds(t * C, C), :].rearrange("p c r -> p (c r)"))\
                    .then_inc(slots_in[b], 16)
                if not first:
                    sp.wait_ge(x2_set, t - 1)
                sp.dma_start(mixed_in[0:T, b, :], mixed[bass.ds(t * T, T), :]).then_inc(rest_in[b], 16)
                sp.dma_start(extra_in[0:T, b, :], extra[bass.ds(t * T, T), :]).then_inc(rest_in[b], 16)

            def store(p, b):
                sp.dma_start(out[bass.ds((2 * p + b) * T, T), :], y[0:T, b, :]).then_inc(y_stored, 16)

            for t in range(4):
                load(t, t % 2, t // 2, t < 2)
            with sp.Fori(0, PAIRS - 2) as p:
                for b in range(2):
                    load(2 * p + 4 + b, b, p + 2)
                sp.wait_ge(y_added, NE * (p + 1))
                for b in range(2):
                    store(p, b)
            load(NT - 1, 0, PAIRS)
            for p in range(PAIRS - 2, PAIRS):
                sp.wait_ge(y_added, NE * (p + 1))
                for b in range(2):
                    store(p, b)
            sp.wait_ge(y_added, NE * (PAIRS + 1))
            store(PAIRS, 0)
            sp.wait_ge(y_stored, 16 * NT)

        @block.gpsimd
        def _(pool):
            pool.iota(iota_row[:, :], [[1, T]], base=0, channel_multiplier=0,
                      allow_small_or_imprecise_dtypes=True).then_inc(consts_set, 1)
            pool.memset(ident[:, :], 0.0).then_inc(consts_set, 1)
            pool.memset(above[:, :], 1.0).then_inc(consts_set, 1)
            pool.wait_ge(consts_set, 3)
            pool.affine_select(out=ident[:, :], in_=ident[:, :], compare_op=ALU.not_equal, fill=1.0,
                               base=0, pattern=[[-1, P]], channel_multiplier=1).then_inc(consts_set, 1)
            pool.affine_select(out=above[:, :], in_=above[:, :], compare_op=ALU.is_gt, fill=0.0,
                               base=0, pattern=[[1, P]], channel_multiplier=-1).then_inc(consts_set, 1)

            pool.wait_ge(zeros_out, 16 * 5)

            def scatter(b, k):
                pool.wait_ge(chunk_in[b], 16 * (k + 1))
                apart(pool, pool_passed)
                for c in range(C):
                    pool.indirect_dma_start(
                        slots, bass.IndirectOffsetOnAxis(ap=rec_buf[:, b, c, 3:4].bitcast(I32), axis=0),
                        rec_buf[:, b, c, :], None, bounds_check=P * NB - 1, oob_is_err=False)\
                        .then_inc(chunk_out[b], 16)

            with pool.Fori(0, CH // 2) as i:
                for b in range(2):
                    scatter(b, i)
            if CH % 2:
                scatter(0, CH // 2)

            pool.wait_ge(stage2_done, 1)
            for b in range(2):
                pool.wait_ge(g_stored[b], 16 * ((NT + 1 - b) // 2))

            over_pool(pool)

            def gather(t, b, k, first=False):
                pool.wait_ge(slots_set, t + 1)
                apart(pool, pool_passed)
                for c in range(C):
                    if not first:
                        pool.wait_ge(block_added, (t - 1) * C + c + 1)
                        apart(pool, pool_passed)
                    pool.indirect_dma_start(
                        rows[:, c, :].bitcast(F32), None, table,
                        bass.IndirectOffsetOnAxis(ap=slot_col[:, b, c:c + 1], axis=0))\
                        .then_inc(row_in[c], 16)

            gather(0, 0, 0, True)
            gather(1, 1, 0)
            with pool.Fori(1, PAIRS) as p:
                for b in range(2):
                    gather(2 * p + b, b, p)
            gather(NT - 1, 0, PAIRS)

        @block.scalar
        def _(act):
            for w, t in ((wq, wq_s), (wk, wk_s), (wv, wv_s), (wo, wo_s), (w_gnn, wg_s)):
                act.dma_start(t[:, :, :], by_chunk(w)).then_inc(small_in, 16)
            for b, t in ((bk, bk_s), (bv, bv_s), (bo, bo_s), (gamma, gamma_s), (beta, beta_s), (br, br_s)):
                act.dma_start(t[:, :], to_rows(b)).then_inc(small_in, 16)
            with nc.allow_non_contiguous_dma(reason="a few thousand numbers, once"):
                act.dma_start(bq_s[:, :], bq.rearrange("(k p) -> p k", p=P)).then_inc(small_in, 16)
                act.dma_start(b1_s[:, :, :], b1.rearrange("e (c p) -> p e c", p=P)).then_inc(small_in, 16)
            act.dma_start(b2_s[:, :], b2).then_inc(small_in, 16)
            act.dma_start(wr_s[:, :, :], by_chunk(Wr)).then_inc(small_in, 16)
            act.wait_ge(small_in, SMALL)

            def load_x(t, b):
                act.dma_start(x_in[0:T, b, :], x[bass.ds(t * T, T), :]).then_inc(x_loaded[b], 16)

            def exp_k(t):
                act.wait_ge(k_zed, t + 1)
                act.activation(k_exp[0:T, :], k_z[0:T, :], ACT.Exp)
                act.activation(k_pos[0:T, :], k_z[0:T, :], ACT.Relu).then_inc(k_exped, 1)

            def sweep1(t, b):
                if has(t + 1):
                    act.wait_ge(xn_turned, t + 2)
                    act.activation(xn_t[:, 1 - b, :, :], xn_tp, ACT.Copy).then_inc(xn_t_set, 1)
                if has(t - 1):
                    exp_k(t - 1)
                if has(t + 4):
                    act.wait_ge(x_normed, t + 3)
                    load_x(t + 4, b)
                act.wait_ge(proj_done, t + 1)
                if not isinstance(t, int) or t:
                    act.wait_ge(q_set, t)
                for c in range(KD):
                    act.activation(q_exp[:, c, :], q_p[b][:, c, :], ACT.Exp, bias=bq_s[:, c:c + 1])
                    m = act.activation(q_pos[:, c, :], q_p[b][:, c, :], ACT.Relu, bias=bq_s[:, c:c + 1])
                m.then_inc(q_exped, 1)
                if not isinstance(t, int) or t >= 2:
                    act.wait_ge(g_stored[b], 8 * t - 8 * b)
                act.activation(g_out[0:T, b, :], g_p[0:T, :], ACT.Copy).then_inc(g_copied, 1)
                act.wait_ge(g_copied, t + 1)
                act.dma_start(table[bass.ds(t * T, T), :], g_out[0:T, b, :]).then_inc(g_stored[b], 16)

            load_x(0, 0)
            load_x(1, 1)
            act.wait_ge(x_normed, 1)
            load_x(2, 0)
            act.wait_ge(x_normed, 2)
            load_x(3, 1)
            act.wait_ge(xn_turned, 1)
            act.activation(xn_t[:, 0, :, :], xn_tp, ACT.Copy).then_inc(xn_t_set, 1)
            over_tiles(act, 0, 2, NT - 5, NT, sweep1)
            exp_k(NT - 1)

            def stage_in(w, b):
                e = bass.ds(w, 1)
                act.dma_start(stage[:, b, :].rearrange("p (k n) -> p k n", k=(KD, HC)[b]),
                              (W1, W2)[b][e, :, :].rearrange("e (k p) n -> p (e k) n", p=P)).then_inc(split_in[b], 16)

            def sweep2(t, b, split=None):
                if has(t - 2):
                    act.wait_ge(mix_set, t - 1)
                    act.dma_start(mixed[bass.ds((t - 2) * T, T), :], mix_out[0:T, 1 - b, :]).then_inc(mix_stored[1 - b], 16)
                if has(t):
                    load_x(t, 1 - b)
                if has(t + 2):
                    if not isinstance(t, int) or t >= 0:
                        act.wait_ge(attn_mm, t + 1)
                    act.activation(q_now[:, b, :, :], q_t[:, :, bass.ds((t + 2) * T, T)], ACT.Copy).then_inc(q_copied, 1)
                if has(t):
                    act.wait_ge(attn_turned, t + 1)
                    if not isinstance(t, int) or t >= 2:
                        act.wait_ge(mix_mm, t - 1)
                    act.activation(attn_t[:, b, :, :], xn_tp, ACT.Copy).then_inc(attn_t_set, 1)
                if split is not None:
                    first = isinstance(split, int) and split == 0
                    last = isinstance(split, int) and split == NE - 1
                    if not (first and b == 0) and not (last and b == 1):
                        act.wait_ge(split_low, 2 * split + b)
                        stage_in(split + b, 1 - b)
                    act.wait_ge(split_in[b], 16 * (split + 1))
                    act.activation((w1h, w2h)[b][:, bass.ds(split, 1), :, :].rearrange("p e k n -> p (e k n)"),
                                   stage[:, b, :], ACT.Copy).then_inc(split_high, 1)

            act.wait_ge(records_set, 2)
            act.wait_ge(zeros_out, 16 * 5)
            for b in range(2):
                stage_in(0, b)
            act.wait_ge(x_normed, NT)
            act.wait_ge(q_set, NT)
            sweep2(-2, 0)
            sweep2(-1, 1)
            for t in range(2):
                sweep2(t, t)
            for t in range(2, 4):
                sweep2(t, t % 2, 0)
            with act.Fori(2, NE) as i:
                sweep2(2 * i, 0, i - 1)
                sweep2(2 * i + 1, 1, i - 1)
            for t in range(2 * NE, 2 * NE + 2):
                sweep2(t, t % 2, NE - 1)
            for t in range(2 * NE + 2, NT + 2):
                sweep2(t, t % 2)
            act.activation(wr_h[:, :, :], wr_s[:, :, :], ACT.Copy).then_inc(wr_split, 1)

            act.wait_ge(q_copied, NT)
            act.activation(weight_h[:, :], rec[:, LO:J, 1], ACT.Copy).then_inc(halved, 1)
            act.wait_ge(halved, 2)

            def place(j, u):
                act.wait_ge(hot_b_set, j + 1)
                if not isinstance(j, int) or j >= DEPTH:
                    act.wait_ge(col_placed, j - DEPTH + 1)
                one = bass.ds(j, 1)
                for f, v in enumerate((weight_h[:, one].bitcast(F32), rec[:, bass.ds(j + LO, 1), 2], weight_l[:, one])):
                    m = act.activation(fields[:, u, f + 1, :], hot_b[:, u, :], ACT.Copy, scale=v)
                m.then_inc(fields_set, 1)

            over_columns(act, place)

            def halves(p):
                act.wait_ge(turned, p + 1)
                act.activation(xf_h[:, :, :].rearrange("p k n -> p (k n)"), misc[:, 0:KD * W2T], ACT.Copy).then_inc(xf_high, 1)

            def high_rows(p, nxt, e):
                blocks, first = part_of(nxt, e)
                for i, (b, c) in enumerate(blocks):
                    t, q = 2 * p + b, first + i
                    if q >= HIGH or not isinstance(p, int) or p:
                        act.wait_ge(block_added, 2 * p * C + max(q - HIGH + 1, 0))
                    act.wait_ge(row_in[c], 16 * (t + 1))
                    act.activation(rows_h[:, q % HIGH, :], rows[:, c, :].bitcast(F32), ACT.Copy,
                                   scale=slot_rec[:, b, c, 1:2]).then_inc(rows_high, 1)

            def expert(p, e, n):
                x_ = p * NE + e
                for c in range(HC):
                    if c % 2 == 0:
                        act.wait_ge(hidden_mm, 2 * x_ + c // 2 + 1)
                        if e or not isinstance(p, int) or p:
                            act.wait_ge(h_split, 2 * x_ + c // 2 - 1 if e or c else 2 * x_)
                    act.activation(h[:, c, 0:n], hp[:, e % 2, c, 0:n], ACT.Gelu,
                                   bias=b1_s[:, e, c:c + 1]).then_inc(h_set, 1)
                    if c % 2:
                        if c == 1 and (e >= 2 or not isinstance(p, int) or p):
                            act.wait_ge(expert_mm, x_ - 1 if e >= 2 else p * NE)
                        act.wait_ge(h_set, HC * x_ + c + 1)
                        act.activation(h_h[:, e % 2, c - 1:c + 1, 0:n], h[:, c - 1:c + 1, 0:n], ACT.Copy).then_inc(h_high, 1)

            def pair(p, tiles, nxt):
                for e in range(NE):
                    expert(p, e, W2T if tiles == 2 else T + 1)
                    if e == 0:
                        act.wait_ge(diff_set, p + 1)
                        act.activation(share[0:T, 0:tiles, 1:2], share[0:T, 0:tiles, 0:1], ACT.Tanh, scale=0.5).then_inc(tanh_set, 1)
                    if e == 2:
                        act.wait_ge(gate_turned, p + 1)
                        act.activation(gate_t[:, 0:tiles, :], misc[0:NE, 0:tiles * T].rearrange("p (b n) -> p b n", b=tiles), ACT.Copy).then_inc(gate_copied, 1)
                    high_rows(p + 1, nxt, e + 1)
                if nxt:
                    halves(p + 1)
                if nxt == 2:
                    high_rows(p + 2, 1, 0)

            for e in range(NE):
                high_rows(0, 2, e)
            halves(0)
            high_rows(1, 2, 0)
            pair(0, 2, 2)
            with act.Fori(1, PAIRS - 1) as p:
                pair(p, 2, 2)
            pair(PAIRS - 1, 2, 1)
            pair(PAIRS, 1, 0)

        @block.tensor
        def _(pe):
            pe.wait_ge(consts_set, 5)
            pe.wait_ge(totals_done, 1)
            pe.matmul(before_p, above[:, :], totals[:, :], start=True, stop=True).then_inc(before_mm, 1)

            pe.wait_ge(over_counted, 1)
            pe.matmul(over_p, over_n[:, :], ones[:, :], start=True, stop=True).then_inc(over_mm, 1)

            pe.wait_ge(small_in, SMALL)

            def turn_xn(t, b):
                pe.wait_ge(x_normed, t + 1)
                if not isinstance(t, int) or t:
                    pe.wait_ge(xn_t_set, t)
                for c in range(KD):
                    m = pe.transpose(xn_tp[:, c, :], xn[0:T, b, c * P:(c + 1) * P], ident[0:T, 0:T])
                m.then_inc(xn_turned, 1)

            def add_kv(t, b, start=False, stop=False):
                pe.wait_ge(k_set, t + 1)
                pe.wait_ge(v_set, t + 2)
                for c in range(KD):
                    m = pe.matmul(kv_p[c], k_map[0:T, b, c * P:(c + 1) * P], v_one[0:T, b, c, :], start=start, stop=stop,
                                  skip_group_check=True)
                m.then_inc(kv_added, 1)

            def sweep1(t, b):
                if has(t + 1):
                    turn_xn(t + 1, 1 - b)
                if has(t - 2):
                    add_kv(t - 2, b, start=isinstance(t, int) and t == 2)
                pe.wait_ge(xn_t_set, t + 1)
                if not isinstance(t, int) or t >= 2:
                    pe.wait_ge(q_set, t - 1)
                    pe.wait_ge(v_set, t)
                if not isinstance(t, int) or t:
                    pe.wait_ge(g_copied, t)
                for c in range(KD):
                    for k in range(KD):
                        pe.matmul(q_p[b][:, c, :], wq_s[:, k, c * P:(c + 1) * P], xn_t[:, b, k, :], start=k == 0, stop=k == KD - 1)
                for o, w in ((k_p[b], wk_s), (v_p[b], wv_s), (g_p, wg_s)):
                    for k in range(KD):
                        m = pe.matmul(o[0:T, :], xn_t[:, b, k, :], w[:, k, :], start=k == 0, stop=k == KD - 1)
                m.then_inc(proj_done, 1)

            turn_xn(0, 0)
            over_tiles(pe, 0, 4, NT - 5, NT, sweep1)
            add_kv(NT - 2, 1)
            add_kv(NT - 1, 0, stop=True)

            def sweep2(t, b):
                if has(t + 1):
                    pe.wait_ge(q_copied, t + 2)
                    if not isinstance(t, int) or t >= 1:
                        pe.wait_ge(attn_set, t)
                    for c in range(KD):
                        m = pe.matmul(attn_p[1 - b][0:T, c, :], q_now[:, 1 - b, c, :], kv_s[:, c, :], start=True, stop=True)
                    m.then_inc(attn_mm, 1)
                if has(t):
                    pe.wait_ge(attn_set, t + 1)
                    if not isinstance(t, int) or t:
                        pe.wait_ge(attn_t_set, t)
                    for c in range(KD):
                        m = pe.transpose(xn_tp[:, c, :], attn[0:T, b, c * P:(c + 1) * P], ident[0:T, 0:T])
                    m.then_inc(attn_turned, 1)
                if has(t - 1):
                    pe.wait_ge(attn_t_set, t)
                    if not isinstance(t, int) or t >= 2:
                        pe.wait_ge(mix_set, t - 1)
                    for k in range(KD):
                        m = pe.matmul(mix_p[0:T, :], attn_t[:, 1 - b, k, :], wo_s[:, k, :], start=k == 0, stop=k == KD - 1)
                    m.then_inc(mix_mm, 1)

            pe.wait_ge(kv_ready, 1)
            sweep2(-1, 1)
            over_tiles(pe, 0, 2, NT - 1, NT + 1, sweep2)

            def place(j, u):
                pe.wait_ge(hot_a_set, j + 1)
                pe.wait_ge(fields_set, j + 1)
                for k in range(WAYS):
                    m = pe.matmul(place_p[k][:, 0:4 * NQ], hot_a[:, u, k * P:(k + 1) * P], fields[:, u, :, :].rearrange("p f n -> p (f n)"),
                                  start=isinstance(j, int) and j == 0, stop=isinstance(j, int) and j == JP - 1,
                                  skip_group_check=True)
                m.then_inc(col_placed, 1)

            over_columns(pe, place)

            pe.wait_ge(stage2_done, 1)
            over_pe(pe)

            def three(o, lh, ll, rh, rl, start, stop):
                pe.matmul(o, lh, rh, start=start, stop=False)
                pe.matmul(o, lh, rl, start=False, stop=False)
                return pe.matmul(o, ll, rh, start=False, stop=stop)

            def add_blocks(p, nxt, e):
                blocks, first = part_of(nxt, e)
                for i, (b, c) in enumerate(blocks):
                    t, q = 2 * p + b, first + i
                    if q == 0 and (not isinstance(p, int) or p):
                        pe.wait_ge(x2_set, 2 * p)
                    if i == 0:
                        pe.wait_ge(onehot_set, SUM_EXPERTS * p + e + 1)
                    pe.wait_ge(rows_low, t * C + c + 1)
                    pe.matmul(agg[0:T, b, :], onehot[:, e % 2, i, :], rows_h[:, q % HIGH, :], start=c == 0, stop=False)
                    pe.matmul(agg[0:T, b, :], onehot[:, e % 2, i, :], rows[:, c, :], start=False, stop=c == C - 1).then_inc(block_added, 1)

            def turn(p, tiles):
                pe.wait_ge(normed, p + 1)
                if not isinstance(p, int) or p:
                    pe.wait_ge(y_begun, p)
                for b in range(tiles):
                    for k in range(KD):
                        m = pe.transpose(misc[:, (k * 2 + b) * T:(k * 2 + b + 1) * T],
                                         z[0:T, b, k * P:(k + 1) * P], ident[0:T, 0:T])
                m.then_inc(turned, 1)

            def hidden(p, e, n):
                x_ = p * NE + e
                if e >= 2:
                    pe.wait_ge(h_set, HC * (x_ - 1))
                for c in range(HC):
                    for k in range(KD):
                        m = three(hp[:, e % 2, c, 0:n], w1h[:, e, k, c * P:(c + 1) * P], w1l[:, e, k, c * P:(c + 1) * P],
                                  xf_h[:, k, 0:n], xf_l[:, k, 0:n], k == 0, k == KD - 1)
                    if c % 2:
                        m.then_inc(hidden_mm, 1)

            def output(p, e, tiles):
                x_ = p * NE + e
                if e >= 2 or not isinstance(p, int) or p:
                    pe.wait_ge(y_added, x_ - 1 if e else x_)
                for b in range(tiles):
                    for c in range(HC):
                        if b == 0 and c % 2 == 0:
                            pe.wait_ge(h_split, 2 * x_ + c // 2 + 1)
                        m = three(yp[0:T, e % 2, b, :], h_h[:, e % 2, c, b * T:(b + 1) * T], h_l[:, e % 2, c, b * T:(b + 1) * T],
                                  w2h[:, e, c, :], w2l[:, e, c, :], c == 0, c == HC - 1)
                m.then_inc(expert_mm, 1)

            def pair(p, tiles, nxt):
                n = W2T if tiles == 2 else T + 1
                pe.wait_ge(xf_high, p + 1)
                pe.wait_ge(xf_low, p + 1)
                for b in range(tiles):
                    for k in range(KD):
                        m = three(misc[0:T, b * NE:(b + 1) * NE], xf_h[:, k, b * T:(b + 1) * T], xf_l[:, k, b * T:(b + 1) * T],
                                  wr_h[:, k, :], wr_l[:, k, :], k == 0, k == KD - 1)
                m.then_inc(logits_mm, 1)
                for e in range(NE):
                    hidden(p, e, n)
                    if e == 2:
                        pe.wait_ge(gate_set, p + 1)
                        for b in range(tiles):
                            m = pe.transpose(misc[0:NE, b * T:(b + 1) * T], gate[0:T, b, :], ident[0:T, 0:T])
                        m.then_inc(gate_turned, 1)
                    add_blocks(p + 1, nxt, e)
                    if e == 2:
                        pe.wait_ge(gate_copied, p + 1)
                        for b in range(tiles):
                            m = pe.matmul(misc[0:T, b * D:(b + 1) * D], gate_t[:, b, :], b2_s[:, :], start=True, stop=True)
                        m.then_inc(bias_mm, 1)
                    if e:
                        output(p, e - 1, tiles)
                if nxt:
                    turn(p + 1, nxt)
                output(p, NE - 1, tiles)

            pe.wait_ge(wr_split, 2)
            pe.wait_ge(split_low, 2 * NE)
            for e in range(NE):
                add_blocks(0, 2, e)
            turn(0, 2)
            pair(0, 2, 2)
            with pe.Fori(1, PAIRS - 1) as p:
                pair(p, 2, 2)
            pair(PAIRS - 1, 2, 1)
            pair(PAIRS, 1, 0)

        @block.vector
        def _(dve):
            s = Steps(dve, dve_step)
            dve.memset(src_i[96:P, LAST:J], N - 1).then_inc(pads_set, 1)
            dve.memset(dst_i[96:P, LAST:J], 0).then_inc(pads_set, 1)
            dve.memset(weight[96:P, LAST:J], 0.0).then_inc(pads_set, 1)
            dve.memset(zeros[:, :], 0.0).then_inc(zeros_set, 1)
            dve.memset(v_one[:, :, :, :], 1.0).then_inc(v_set, 1)
            dve.memset(kv_s[:, :, :], 0.0).then_inc(pads_set, 1)
            dve.wait_ge(edges_in, 16 * 6)

            dve.tensor_copy(rec[:, :, 1], weight[:, :])
            dve.tensor_copy(rec[:, :, 2], dst_i[:, :])
            s(dve.tensor_copy(src_f[:, :], src_i[:, :]))
            s(dve.tensor_scalar(tile_i[:, :], src_f[:, :], 1.0 / T, 0.5 / T, ALU.mult, ALU.add))
            s(dve.tensor_copy(tile_f[:, :], tile_i[:, :]))
            s(dve.scalar_tensor_tensor(rest[:, :], tile_f[:, :], -float(T), src_f[:, :], ALU.mult, ALU.add))
            s(dve.scalar_tensor_tensor(tile_f[:, :], rest[:, :], float(T), tile_f[:, :], ALU.is_ge, ALU.add))
            s(dve.scalar_tensor_tensor(tile_f[:, :], rest[:, :], 0.0, tile_f[:, :], ALU.is_ge, ALU.add))
            s(dve.tensor_scalar(tile_f[:, :], tile_f[:, :], -1.0, None, ALU.add))
            s(dve.scalar_tensor_tensor(rec[:, :, 0], tile_f[:, :], -float(T), src_f[:, :], ALU.mult, ALU.add))
            for t in range(NT):
                m = dve.tensor_scalar(mask[:, t, :], tile_f[:, :], float(t), None, ALU.is_equal)
            s(m)
            for t in range(NT):
                m = dve.tensor_tensor_scan(seen[:, t, :], mask[:, t, :], zeros[:, 0:J], 0.0, ALU.add, ALU.add)
            s(m)
            dve.tensor_copy(totals[:, :], seen[:, :, J - 1]).then_inc(totals_done, 1)
            dve.wait_ge(before_mm, 1)
            s(dve.tensor_scalar(before[:, :], before_p, -1.0, None, ALU.add))
            def slots_of(lo, hi):
                n = hi - lo
                now, to = seen[:, :, lo:hi], mask[:, :, lo:hi]
                s(dve.tensor_tensor(now, now, before[:, :].unsqueeze(2).to_broadcast([P, NT, n]), ALU.add))
                s(dve.tensor_tensor(to, now, to, ALU.mult))
                s(dve.tensor_reduce(rank[:, lo:hi], to.rearrange("p t j -> p j t"), AX.X, ALU.add))
                s(dve.scalar_tensor_tensor(over_w[:, lo:hi], rank[:, lo:hi], float(CAP), rec[:, lo:hi, 1], ALU.is_ge, ALU.mult))
                s(dve.tensor_copy(tile_i[:, lo:hi], rank[:, lo:hi]))
                s(dve.tensor_scalar(src_i[:, lo:hi], tile_i[:, lo:hi], 7, None, ALU.logical_shift_right))
                s(dve.tensor_scalar(tile_i[:, lo:hi], tile_i[:, lo:hi], P - 1, None, ALU.bitwise_and))
                s(dve.scalar_tensor_tensor(rest[:, lo:hi], tile_f[:, lo:hi], float(C), src_i[:, lo:hi], ALU.mult, ALU.add))
                s(dve.scalar_tensor_tensor(tile_f[:, lo:hi], tile_i[:, lo:hi], float(NB), rest[:, lo:hi], ALU.mult, ALU.add))
                s(dve.tensor_scalar(rank[:, lo:hi], rank[:, lo:hi], float(CAP), float(2 * P * NB), ALU.is_ge, ALU.mult))
                dve.tensor_tensor(rec[:, lo:hi, 3].bitcast(I32), tile_f[:, lo:hi], rank[:, lo:hi], ALU.add).then_inc(records_set, 1)

            slots_of(0, 2 * C)
            slots_of(2 * C, J)
            s(dve.tensor_copy(src_i[:, LO:J], rest[:, LO:J]))
            s(dve.tensor_scalar(dst_i[:, LO:J], src_i[:, LO:J], WAYS - 1, None, ALU.bitwise_and))
            s(dve.tensor_scalar(src_i[:, LO:J], src_i[:, LO:J], WAYS.bit_length() - 1, None, ALU.logical_shift_right))
            s(dve.tensor_tensor(slot_b[:, :], src_i[:, LO:J], rank[:, LO:J], ALU.add))
            s(dve.scalar_tensor_tensor(slot_a[:, :], dst_i[:, LO:J], float(P), tile_i[:, LO:J], ALU.mult, ALU.add))
            dve.memset(ones[:, :], 1.0)
            dve.tensor_reduce(over_n[:, :], rank[:, :], AX.X, ALU.max).then_inc(over_counted, 1)
            dve.wait_ge(over_mm, 1)
            dve.tensor_scalar(over_any[:, :], over_p, 1.0, None, ALU.min).then_inc(over_set, 1)
            done = s.n

            dve.wait_ge(small_in, SMALL)
            S1 = 2 + RSQRT_STEPS + 1

            def moments_x(k, n):
                s = Steps(dve, dve_step, done + k * S1)
                for b in range(n):
                    dve.wait_ge(x_loaded[b], 16 * (k + 1))
                    m = dve.bn_stats(stat1[0:T, b, :], x_in[0:T, b, :])
                s(m, dve_passed)
                for b in range(n):
                    m = dve.bn_aggr(mv1[0:T, b, :], stat1[0:T, b, :])
                s(m)
                s(dve.tensor_scalar(rs1[0:T, 0, 0:n], mv1[0:T, 0:n, 1], EPS, None, ALU.add))
                rsqrt(dve, s, rs1[0:T, 0, 0:n], rs1[0:T, 1, 0:n], rs1[0:T, 2, 0:n])
                assert s.n == S1

            def norm_x(t, b):
                if not isinstance(t, int) or t >= 2:
                    dve.wait_ge(xn_turned, t - 1)
                dve.tensor_scalar(xn[0:T, b, :], x_in[0:T, b, :], mv1[0:T, b, 0:1], rs1[0:T, 1, b:b + 1], ALU.subtract, ALU.mult).then_inc(x_normed, 1)

            def map_k(t, b):
                dve.wait_ge(k_exped, t + 1)
                if not isinstance(t, int) or t >= 2:
                    dve.wait_ge(kv_added, t - 1)
                dve.scalar_tensor_tensor(k_map[0:T, b, :], k_exp[0:T, :], 1.0, k_pos[0:T, :], ALU.min, ALU.add).then_inc(k_set, 1)

            def sweep1(t, b, k=None):
                k = t // 2 if isinstance(t, int) else k
                if has(t - 1):
                    map_k(t - 1, 1 - b)
                dve.wait_ge(proj_done, t + 1)
                if not isinstance(t, int) or t:
                    dve.wait_ge(k_set, t)
                dve.tensor_tensor(k_z[0:T, :], k_p[b][0:T, :], bk_s[0:T, :], ALU.add).then_inc(k_zed, 1)
                if not isinstance(t, int) or t >= 2:
                    dve.wait_ge(kv_added, t - 1)
                dve.tensor_tensor(v_one[0:T, b, :, 0:P], v_p[b][0:T, :].rearrange("p (c n) -> p c n", c=KD),
                                  bv_s[0:T, :].rearrange("p (c n) -> p c n", c=KD), ALU.add).then_inc(v_set, 1)
                dve.wait_ge(q_exped, t + 1)
                dve.scalar_tensor_tensor(q_t[:, :, bass.ds(t * T, T)], q_exp[:, :, :], 1.0, q_pos[:, :, :], ALU.min, ALU.add).then_inc(q_set, 1)
                if has(t + 3):
                    if b == 1:
                        dve.wait_ge(x_normed, t + 3)
                        moments_x(k + 2, 2 if has(t + 4) else 1)
                    norm_x(t + 3, 1 - b)

            moments_x(0, 2)
            norm_x(0, 0)
            norm_x(1, 1)
            dve.wait_ge(x_normed, 2)
            moments_x(1, 2)
            norm_x(2, 0)
            for t in range(2):
                sweep1(t, t)
            with dve.Fori(1, (NT - 5) // 2) as i:
                sweep1(2 * i, 0, i)
                sweep1(2 * i + 1, 1, i)
            for t in range(NT - 5, NT):
                sweep1(t, t % 2)
            map_k(NT - 1, 0)
            done = done + (NT + 1) // 2 * S1

            dve.wait_ge(kv_added, NT)
            for c in range(KD):
                for g in range(P // HD):
                    r = slice(g * HD, (g + 1) * HD)
                    dve.tensor_copy(kv_s[r, c, r], kv_p[c][r, r])
                    m = dve.tensor_copy(kv_s[r, c, P + g:P + g + 1], kv_p[c][r, P:P + 1])
            m.then_inc(kv_ready, 1)

            S2 = 1

            def sweep2(t, b, k=None, split=None):
                k = t // 2 if isinstance(t, int) else k
                if has(t + 1):
                    s = Steps(dve, dve_step, done + (t + 1) * S2)
                    dve.wait_ge(attn_mm, t + 2)
                    if not isinstance(t, int) or t >= 0:
                        dve.wait_ge(attn_set, t + 1)
                    now = attn_p[1 - b]
                    s(dve.tensor_scalar(norm[0:T, :].rearrange("p (c g) -> p c g", c=KD), now[0:T, :, P:NK], 1e-6, None, ALU.add))
                    assert s.n == S2
                    dve.reciprocal(norm[0:T, :], norm[0:T, :]).then_inc(norm_set, 1)
                    dve.wait_ge(norm_set, t + 2)
                    if not isinstance(t, int) or t >= 1:
                        dve.wait_ge(attn_turned, t)
                    for c in range(KD):
                        g = P // HD
                        m = dve.tensor_tensor(attn[0:T, 1 - b, c * P:(c + 1) * P].rearrange("p (g d) -> p g d", g=g),
                                              now[0:T, c, 0:P].rearrange("p (g d) -> p g d", g=g),
                                              norm[0:T, c * g:(c + 1) * g].unsqueeze(2).to_broadcast([T, g, HD]), ALU.mult)
                    m.then_inc(attn_set, 1)
                if has(t - 1):
                    dve.wait_ge(x_loaded[b], 16 * ((NT + 1) // 2 + k if b == 0 else NT // 2 + k + 1))
                    dve.tensor_tensor(x_in[0:T, b, :], x_in[0:T, b, :], bo_s[0:T, :], ALU.add).then_inc(x_biased, 1)
                    dve.wait_ge(x_biased, t)
                    dve.wait_ge(mix_mm, t)
                    if not isinstance(t, int) or t >= 3:
                        dve.wait_ge(mix_stored[b], 16 * (k - 1 + b))
                    dve.tensor_tensor(mix_out[0:T, b, :], mix_p[0:T, :], x_in[0:T, b, :], ALU.add).then_inc(mix_set, 1)
                if split is not None:
                    wh, wl = ((w1h, w1l), (w2h, w2l))[b]
                    dve.wait_ge(split_high, 2 * split + b + 1)
                    dve.tensor_tensor(wl[:, bass.ds(split, 1), :, :].rearrange("p e k n -> p (e k n)"), stage[:, b, :],
                                      wh[:, bass.ds(split, 1), :, :].rearrange("p e k n -> p (e k n)").bitcast(F32),
                                      ALU.subtract).then_inc(split_low, 1)

            sweep2(-1, 1)
            for t in range(2):
                sweep2(t, t)
            with dve.Fori(1, NE) as i:
                sweep2(2 * i, 0, i, i - 1)
                sweep2(2 * i + 1, 1, i, i - 1)
            for t in range(2 * NE, 2 * NE + 2):
                sweep2(t, t % 2, split=NE - 1)
            for t in range(2 * NE + 2, NT + 1):
                sweep2(t, t % 2)
            done = done + NT * S2
            dve.wait_ge(wr_split, 1)
            dve.tensor_tensor(wr_l[:, :, :], wr_s[:, :, :], wr_h[:, :, :].bitcast(F32), ALU.subtract).then_inc(wr_split, 1)

            dve.wait_ge(q_copied, NT)
            s = Steps(dve, dve_step, done)
            for a in range(0, WAYS * P, T):
                n = min(T, WAYS * P - a)
                m = dve.tensor_scalar(iota_a[:, a:a + n], iota_row[:, 0:n], float(a), None, ALU.add)
            s(m)
            done = done + s.n
            dve.wait_ge(halved, 1)
            dve.tensor_tensor(weight_l[:, :], rec[:, LO:J, 1], weight_h[:, :].bitcast(F32), ALU.subtract).then_inc(halved, 1)

            def place(j, u):
                if not isinstance(j, int) or j >= DEPTH:
                    dve.wait_ge(col_placed, j - DEPTH + 1)
                one = bass.ds(j, 1)
                dve.tensor_scalar(hot_b[:, u, :], iota_a[:, 0:NQ], slot_b[:, one], None, ALU.is_equal).then_inc(hot_b_set, 1)
                dve.tensor_scalar(fields[:, u, 0, :], iota_a[:, 0:NQ], slot_b[:, one], rec[:, bass.ds(j + LO, 1), 0],
                                  ALU.is_equal, ALU.mult)
                dve.tensor_scalar(hot_a[:, u, :], iota_a[:, :], slot_a[:, one], None, ALU.is_equal).then_inc(hot_a_set, 1)

            over_columns(dve, place)
            dve.wait_ge(col_placed, JP)
            for k in range(WAYS):
                m = dve.tensor_copy(sums[:, :, k, :], place_p[k][:, 0:4 * NQ].rearrange("p (f q) -> p q f", f=4))
            m.then_inc(sums_set, 1)

            dve.wait_ge(sums_out, 16)
            dve.wait_ge(mix_stored[0], 16 * (NT // 2))
            dve.wait_ge(mix_stored[1], 16 * (NT // 2 + 1))
            dve.wait_ge(chunk_out[0], 16 * C * (CH - CH // 2))
            dve.wait_ge(chunk_out[1], 16 * C * (CH // 2))
            dve.memset(mv[:, :, :], 0.0).then_inc(stage2_done, 1)

            over_dve(dve)

            def records(t, b, k):
                dve.wait_ge(slots_in[b], 32 * (k + 1))
                dve.tensor_tensor(slot_rec[:, b, :, 0:3], slot_rec[:, b, :, 0:3], slot_more[:, b, :, 0:3], ALU.add).then_inc(slots_summed, 1)
                dve.wait_ge(slots_summed, t + 1)
                dve.tensor_tensor(slot_rec[:, b, :, 1], slot_rec[:, b, :, 1], slot_more[:, b, :, 3], ALU.add)
                dve.tensor_copy(slot_col[:, b, :], slot_rec[:, b, :, 2]).then_inc(slots_set, 1)

            def low_rows(p, nxt, e):
                blocks, first = part_of(nxt, e)
                for b in sorted({b for b, c in blocks}):
                    cs = [c for b_, c in blocks if b_ == b]
                    i, n = blocks.index((b, cs[0])), len(cs)
                    if cs[0] == 0:
                        dve.wait_ge(slots_set, 2 * p + b + 1)
                    if i == 0 and (e >= 2 or not isinstance(p, int) or p):
                        dve.wait_ge(block_added, 2 * p * C + max(e - 1, 0) * PART)
                    m = dve.tensor_tensor(onehot[:, e % 2, i:i + n, :], iota_row[:, :].unsqueeze(1).to_broadcast([P, n, T]),
                                          slot_rec[:, b, cs[0]:cs[-1] + 1, 0:1].to_broadcast([P, n, T]), ALU.is_equal)
                if blocks:
                    m.then_inc(onehot_set, 1)
                for b, c in blocks:
                    dve.wait_ge(rows_high, (2 * p + b) * C + c + 1)
                    dve.scalar_tensor_tensor(rows[:, c, :], rows[:, c, :].bitcast(F32), slot_rec[:, b, c, 1:2],
                                             rows_h[:, (first + blocks.index((b, c))) % HIGH, :].bitcast(F32),
                                             ALU.mult, ALU.subtract).then_inc(rows_low, 1)

            def norms(p, tiles, s, part):
                if part == 0:
                    dve.wait_ge(block_added, (2 * p + tiles) * C)
                    for b in range(tiles):
                        dve.wait_ge(rest_in[b], 32 * (p + 1))
                        m = dve.tensor_tensor(z[0:T, b, :], agg[0:T, b, :], extra_in[0:T, b, :], ALU.add)
                    s(m)
                    for b in range(tiles):
                        dve.scalar_tensor_tensor(x2[0:T, b, :], z[0:T, b, :], 0.0, mixed_in[0:T, b, :], ALU.max, ALU.add).then_inc(x2_set, 1)
                    dve.wait_ge(x2_set, 2 * p + tiles)
                    for b in range(tiles):
                        m = dve.bn_stats(stat[0:T, b, :], x2[0:T, b, :])
                    s(m, dve_passed)
                    for b in range(tiles):
                        m = dve.bn_aggr(mv[0:T, b, :], stat[0:T, b, :])
                    s(m)
                    s(dve.tensor_scalar(rs[0:T, 0, :], mv[0:T, :, 1], 1.0 + EPS, EPS * EPS, ALU.mult, ALU.add))
                if part == 1:
                    rsqrt(dve, s, rs[0:T, 0, :], rs[0:T, 1, :], rs[0:T, 2, :])
                    for b in range(tiles):
                        m = dve.scalar_tensor_tensor(z[0:T, b, :], x2[0:T, b, :], mv[0:T, b, 0:1], gamma_s[0:T, :], ALU.subtract, ALU.mult)
                    s(m)
                    for b in range(tiles):
                        m = dve.scalar_tensor_tensor(z[0:T, b, :], z[0:T, b, :], rs[0:T, 1, b:b + 1], beta_s[0:T, :], ALU.mult, ALU.add)
                    m.then_inc(normed, 1)

            NORM_STEPS = 5 + RSQRT_STEPS

            def low_halves(p):
                dve.wait_ge(xf_high, p + 1)
                dve.tensor_tensor(xf_l[:, :, :].rearrange("p k n -> p (k n)"), misc[:, 0:KD * W2T],
                                  xf_h[:, :, :].rearrange("p k n -> p (k n)").bitcast(F32), ALU.subtract).then_inc(xf_low, 1)

            ROUTE = 10

            def route(p, tiles, s, part):
                if part == 0:
                    dve.wait_ge(logits_mm, p + 1)
                    s(dve.tensor_tensor(logit[0:T, 0:tiles, :], misc[0:T, 0:tiles * NE].rearrange("p (b e) -> p b e", b=tiles),
                                        br_s[0:T, :].unsqueeze(1).to_broadcast([T, tiles, NE]), ALU.add), dve_passed)
                    for b in range(tiles):
                        m = dve.max(top[0:T, b, :], logit[0:T, b, :])
                    s(m)
                    dve.tensor_tensor(share[0:T, 0:tiles, 0:1], top[0:T, 0:tiles, 0:1], top[0:T, 0:tiles, 1:2],
                                      ALU.subtract).then_inc(diff_set, 1)
                    for b in range(tiles):
                        m = dve.max_index(top_at[0:T, b, :], top[0:T, b, :], logit[0:T, b, :])
                    s(m)
                    s(dve.tensor_copy(top_f[0:T, 0:tiles, 0:2], top_at[0:T, 0:tiles, 0:2]))
                else:
                    dve.wait_ge(tanh_set, p + 1)
                    dve.tensor_scalar(share[0:T, 0:tiles, 2:3], share[0:T, 0:tiles, 1:2], 0.5, 0.5, ALU.mult, ALU.add)
                    s(dve.tensor_scalar(share[0:T, 0:tiles, 3:4], share[0:T, 0:tiles, 1:2], -0.5, 0.5, ALU.mult, ALU.add))
                    for b in range(tiles):
                        m = dve.tensor_scalar(gate[0:T, b, :], iota_row[0:T, 0:NE], top_f[0:T, b, 0:1], share[0:T, b, 2:3],
                                              ALU.is_equal, ALU.mult)
                    s(m)
                    for b in range(tiles):
                        m = dve.tensor_scalar(logit[0:T, b, :], iota_row[0:T, 0:NE], top_f[0:T, b, 1:2], share[0:T, b, 3:4],
                                              ALU.is_equal, ALU.mult)
                    s(m)
                    dve.tensor_tensor(gate[0:T, 0:tiles, :], gate[0:T, 0:tiles, :], logit[0:T, 0:tiles, :], ALU.add).then_inc(gate_set, 1)
                    dve.wait_ge(gate_set, p + 1)

            ROUTE_STEPS = 7

            def split(p, e, n):
                x_ = p * NE + e
                if e >= 2:
                    dve.wait_ge(expert_mm, x_ - 1)
                for g in range(2):
                    r = slice(2 * g, 2 * g + 2)
                    dve.wait_ge(h_high, 2 * x_ + g + 1)
                    dve.tensor_tensor(h_l[:, e % 2, r, 0:n], h[:, r, 0:n], h_h[:, e % 2, r, 0:n].bitcast(F32), ALU.subtract).then_inc(h_split, 1)

            def begin_y(p, tiles):
                dve.wait_ge(bias_mm, p + 1)
                if not isinstance(p, int) or p:
                    dve.wait_ge(y_stored, 16 * 2 * p)
                dve.tensor_tensor(y[0:T, 0:tiles, :], misc[0:T, 0:tiles * D].rearrange("p (b n) -> p b n", b=tiles),
                                  x2[0:T, 0:tiles, :], ALU.add).then_inc(y_begun, 1)
                dve.wait_ge(y_begun, p + 1)

            def add_y(p, e, tiles):
                x_ = p * NE + e
                dve.wait_ge(expert_mm, x_ + 1)
                for b in range(tiles):
                    m = dve.scalar_tensor_tensor(y[0:T, b, :], yp[0:T, e % 2, b, :], gate[0:T, b, e:e + 1], y[0:T, b, :],
                                                 ALU.mult, ALU.add)
                m.then_inc(y_added, 1)
                dve.wait_ge(y_added, x_ + 1)

            def pair(p, tiles, nxt, s):
                n = W2T if tiles == 2 else T + 1
                if nxt == 2:
                    records(2 * p + 3, 1, p + 1)
                for e in range(NE):
                    if e == 0:
                        route(p, tiles, s, 0)
                    split(p, e, n)
                    low_rows(p + 1, nxt, e + 1)
                    if e == 0:
                        route(p, tiles, s, 1)
                    if nxt == 2 and e == 3:
                        records(2 * p + 4, 0, p + 2)
                    if e == 2:
                        begin_y(p, tiles)
                        add_y(p, 0, tiles)
                    if e >= 2:
                        add_y(p, e - 1, tiles)
                    if nxt and 0 <= e - NORM_FROM < 2:
                        norms(p + 1, nxt, s, e - NORM_FROM)
                if nxt:
                    low_halves(p + 1)
                if nxt == 2:
                    low_rows(p + 2, 1, 0)
                add_y(p, NE - 1, tiles)

            s = Steps(dve, dve_step, done)
            records(0, 0, 0)
            records(1, 1, 0)
            for e in range(NE):
                low_rows(0, 2, e)
            records(2, 0, 1)
            for part in range(2):
                norms(0, 2, s, part)
            low_halves(0)
            low_rows(1, 2, 0)
            done = done + s.n
            PER = ROUTE_STEPS + NORM_STEPS
            s = Steps(dve, dve_step, done)
            pair(0, 2, 2, s)
            with dve.Fori(1, PAIRS - 1) as p:
                s = Steps(dve, dve_step, done + p * PER)
                pair(p, 2, 2, s)
                assert s.n == PER, s.n
            done = done + (PAIRS - 1) * PER
            s = Steps(dve, dve_step, done)
            pair(PAIRS - 1, 2, 1, s)
            pair(PAIRS, 1, 0, s)


_INS = ["x", "src", "dst", "edge_weight", "L0_gnn_weight", "L0_mix_wq", "L0_mix_bq", "L0_mix_wk", "L0_mix_bk",
        "L0_mix_wv", "L0_mix_bv", "L0_mix_wo", "L0_mix_bo", "L0_ffn_gamma", "L0_ffn_beta", "L0_ffn_Wr",
        "L0_ffn_br", "L0_ffn_W1", "L0_ffn_b1", "L0_ffn_W2", "L0_ffn_b2"]


def kernel(**inputs):
    import numpy as _np
    import concourse.bacc as _bacc
    from concourse import mybir as _mybir
    from concourse.bass_utils import run_bass_kernel_spmd as _run

    nc = _bacc.Bacc("TRN2", target_bir_lowering=False, num_devices=1)
    arrays, args = {}, []
    for name in _INS:
        a = _np.ascontiguousarray(inputs[name])
        arrays[f"in_{name}"] = a
        args.append(nc.dram_tensor(f"in_{name}", a.shape, _mybir.dt.from_np(a.dtype), kind="ExternalInput").ap())
    args.append(nc.dram_tensor("out_0", (N, D), F32, kind="ExternalOutput").ap())
    build(nc, *args)
    r = _run(nc, [arrays], core_ids=[0])
    return r.results[0]["out_0"]
```
